# Optimizing a Trainium2 kernel written in Bass

```python
import numpy as np
import jax
import jax.numpy as jnp

def _softmax(x, axis=-1):
    return jax.nn.softmax(x, axis=axis)

def _gelu(x):
    return jax.nn.gelu(x, approximate=True)

def _silu(x):
    return jax.nn.silu(x)

def _sigmoid(x):
    return jax.nn.sigmoid(x)

def _layernorm(x, axis=-1, eps=1e-05):
    m = jnp.mean(x, axis=axis, keepdims=True)
    v = jnp.var(x, axis=axis, keepdims=True)
    return (x - m) / jnp.sqrt(v + eps)

def _scatter_add(tgt, idx, src, axis=0):
    return tgt.at[idx].add(src)

def _segment_sum(src, seg, n):
    return jax.ops.segment_sum(src, seg, n)
kernel_name = 'mk_cond_resid_d4_seqx_r8_82753c'

def setup_inputs(seed: int=0):
    np.random.seed(seed)
    _w = jnp.asarray

    def _rec_inputs():
        import jax
        import jax.numpy as jnp
        _rk = jax.random.key(seed)
        x = -7.109e-05 + 0.9999 * jax.random.normal(jax.random.fold_in(_rk, 1), (128, 32, 256), jnp.float32)
        _lenS = 32 - jax.random.randint(jax.random.fold_in(_rk, 7), (128,), 0, max(1, 32 // 4) + 1, jnp.int32)
        _lenS2 = 32 - jax.random.randint(jax.random.fold_in(_rk, 8), (128,), 0, max(1, 32 // 4) + 1, jnp.int32)
        itok_B_1_198 = jax.random.randint(jax.random.fold_in(_rk, 11), (128,), 1, 199, jnp.int32)
        itok_Bx257_0_4111 = jax.random.randint(jax.random.fold_in(_rk, 12), (128, 257), 0, 514, jnp.int32)
        itok_B_37_3939 = jax.random.randint(jax.random.fold_in(_rk, 13), (128,), 37, 3940, jnp.int32)
        itok_B_0_7 = jax.random.randint(jax.random.fold_in(_rk, 14), (128,), 0, 8, jnp.int32)
        fside_8xS_0 = -0.00162727 + 0.0609077 * jax.random.normal(jax.random.fold_in(_rk, 15), (8, 32), jnp.float32)
        return (x, itok_B_1_198, itok_Bx257_0_4111, itok_B_37_3939, itok_B_0_7, fside_8xS_0)
    x, itok_B_1_198, itok_Bx257_0_4111, itok_B_37_3939, itok_B_0_7, fside_8xS_0 = _rec_inputs()

    def _L0_cond_setup():
        import jax, jax.numpy as jnp
        import numpy as np
        B, C, T = (128, 32, 256)
        S, D = (200, 32)
        key = jax.random.key(seed)
        k1, k2, k3 = jax.random.split(key, 3)
        x = jax.random.normal(k1, (B, C, T), dtype=jnp.float32)
        conditions = jax.random.randint(k2, (B,), 0, S, dtype=jnp.int64)
        weights = jax.random.normal(k3, (S, C, D), dtype=jnp.float32) / jnp.sqrt(jnp.float32(C))
        return {'x': x, 'conditions': conditions, 'weights': weights}
    _L0_cond_all = _L0_cond_setup()
    _L0_cond_in = {k: v for k, v in _L0_cond_all.items() if k in ('weights',)}
    del _L0_cond_all

    def _L1_cond_setup():
        import jax, jax.numpy as jnp
        import numpy as np
        H, G, HD = (8, 4, 32)
        GSZ = H // G
        BLOCK = 16
        WINDOW = 128
        SCALE = 256.0 ** (-0.5)
        EPS = 1e-06
        THETA = 10000.0
        B, T, D = (16, 4, 256)
        NBLK = 257

        def _rms(x, scale):
            var = jnp.mean(x * x, axis=-1, keepdims=True)
            return x * jax.lax.rsqrt(var + EPS) * (1.0 + scale)

        def _rope(x, pos):
            half = HD // 2
            inv = 1.0 / THETA ** (jnp.arange(half, dtype=jnp.float32) / half)
            ang = pos[:, :, None].astype(jnp.float32) * inv
            cos = jnp.cos(ang)[:, None, :, :]
            sin = jnp.sin(ang)[:, None, :, :]
            x1, x2 = (x[..., :half], x[..., half:])
            return jnp.concatenate([x1 * cos - x2 * sin, x2 * cos + x1 * sin], axis=-1)
        key = jax.random.key(seed)
        ks = jax.random.split(key, 10)
        inv_d = 1.0 / np.sqrt(D)
        return {'x': jax.random.normal(ks[0], (B, T, D), jnp.float32), 'Wq': jax.random.normal(ks[1], (H * HD, D), jnp.float32) * inv_d, 'Wk': jax.random.normal(ks[2], (G * HD, D), jnp.float32) * inv_d, 'Wv': jax.random.normal(ks[3], (G * HD, D), jnp.float32) * inv_d, 'Wo': jax.random.normal(ks[4], (D, H * HD), jnp.float32) * inv_d, 'q_norm_scale': jax.random.normal(ks[5], (HD,), jnp.float32) * 0.02, 'k_norm_scale': jax.random.normal(ks[6], (HD,), jnp.float32) * 0.02, 'k_blocks': jax.random.normal(ks[7], (B * NBLK, G, BLOCK, HD), jnp.float32), 'v_blocks': jax.random.normal(ks[8], (B * NBLK, G, BLOCK, HD), jnp.float32), 'block_tables': jnp.arange(B * NBLK, dtype=jnp.int32).reshape(B, NBLK), 'kv_lens': jax.random.randint(ks[9], (B,), 0, 512, dtype=jnp.int32)}
    _L1_cond_all = _L1_cond_setup()
    _L1_cond_in = {k: v for k, v in _L1_cond_all.items() if k in ('Wq', 'Wk', 'Wv', 'Wo', 'q_norm_scale', 'k_norm_scale', 'k_blocks', 'v_blocks')}
    del _L1_cond_all

    def _L2_cond_setup():
        import jax, jax.numpy as jnp
        import numpy as np
        B, C, D, T, N_SUBJECTS = (128, 32, 32, 256, 8)
        key = jax.random.key(seed)
        kx, ks, kw = jax.random.split(key, 3)
        x = jax.random.normal(kx, (B, C, T), dtype=jnp.float32)
        subjects = jax.random.randint(ks, (B,), 0, N_SUBJECTS, dtype=jnp.int64)
        weights = jax.random.normal(kw, (N_SUBJECTS, C, D), dtype=jnp.float32) * (1.0 / C ** 0.5)
        return {'x': x, 'subjects': subjects, 'weights': weights}
    _L2_cond_all = _L2_cond_setup()
    _L2_cond_in = {k: v for k, v in _L2_cond_all.items() if k in ('weights',)}
    del _L2_cond_all

    def _L3_cond_setup():
        import jax, jax.numpy as jnp
        import numpy as np
        B, C, T = (64, 32, 256)
        D, N = (32, 8)
        key = jax.random.key(seed)
        k_x, k_s, k_w, k_b = jax.random.split(key, 4)
        scale = 1.0 / np.sqrt(C)
        x = jax.random.normal(k_x, (B, C, T), dtype=jnp.float32)
        subjects = jax.random.randint(k_s, (B,), 0, N, dtype=jnp.int64)
        weights = jax.random.normal(k_w, (N, C, D), dtype=jnp.float32) * scale
        bias = jax.random.normal(k_b, (N, D), dtype=jnp.float32) * scale
        return {'x': x, 'subjects': subjects, 'weights': weights, 'bias': bias}
    _L3_cond_all = _L3_cond_setup()
    _L3_cond_in = {k: v for k, v in _L3_cond_all.items() if k in ('weights',)}
    del _L3_cond_all
    return {'x': x, 'itok_B_1_198': itok_B_1_198, 'itok_Bx257_0_4111': itok_Bx257_0_4111, 'itok_B_37_3939': itok_B_37_3939, 'itok_B_0_7': itok_B_0_7, 'fside_8xS_0': fside_8xS_0, 'L0_cond_weights': _L0_cond_in['weights'], 'L1_cond_Wq': _L1_cond_in['Wq'], 'L1_cond_Wk': _L1_cond_in['Wk'], 'L1_cond_Wv': _L1_cond_in['Wv'], 'L1_cond_Wo': _L1_cond_in['Wo'], 'L1_cond_q_norm_scale': _L1_cond_in['q_norm_scale'], 'L1_cond_k_norm_scale': _L1_cond_in['k_norm_scale'], 'L1_cond_k_blocks': _L1_cond_in['k_blocks'], 'L1_cond_v_blocks': _L1_cond_in['v_blocks'], 'L2_cond_weights': _L2_cond_in['weights'], 'L3_cond_weights': _L3_cond_in['weights']}

def reference(x, itok_B_1_198, itok_Bx257_0_4111, itok_B_37_3939, itok_B_0_7, fside_8xS_0, L0_cond_weights, L1_cond_Wq, L1_cond_Wk, L1_cond_Wv, L1_cond_Wo, L1_cond_q_norm_scale, L1_cond_k_norm_scale, L1_cond_k_blocks, L1_cond_v_blocks, L2_cond_weights, L3_cond_weights):
    import jax
    import jax.numpy as jnp

    def _L0_cond_ref(x, conditions, weights):
        import jax, jax.numpy as jnp
        import numpy as np
        B, C, T = (128, 32, 256)
        S, D = (200, 32)
        w = weights[conditions]
        return jnp.einsum('bct,bcd->bdt', x, w)

    def _L1_cond_ref(x, Wq, Wk, Wv, Wo, q_norm_scale, k_norm_scale, k_blocks, v_blocks, block_tables, kv_lens):
        import jax, jax.numpy as jnp
        import numpy as np
        H, G, HD = (8, 4, 32)
        GSZ = H // G
        BLOCK = 16
        WINDOW = 128
        SCALE = 256.0 ** (-0.5)
        EPS = 1e-06
        THETA = 10000.0
        B, T, D = (16, 4, 256)
        NBLK = 257

        def _rms(x, scale):
            var = jnp.mean(x * x, axis=-1, keepdims=True)
            return x * jax.lax.rsqrt(var + EPS) * (1.0 + scale)

        def _rope(x, pos):
            half = HD // 2
            inv = 1.0 / THETA ** (jnp.arange(half, dtype=jnp.float32) / half)
            ang = pos[:, :, None].astype(jnp.float32) * inv
            cos = jnp.cos(ang)[:, None, :, :]
            sin = jnp.sin(ang)[:, None, :, :]
            x1, x2 = (x[..., :half], x[..., half:])
            return jnp.concatenate([x1 * cos - x2 * sin, x2 * cos + x1 * sin], axis=-1)
        Bx, Tx, _ = x.shape
        q = jnp.einsum('btd,od->bto', x, Wq).reshape(Bx, Tx, H, HD).transpose(0, 2, 1, 3)
        k = jnp.einsum('btd,od->bto', x, Wk).reshape(Bx, Tx, G, HD).transpose(0, 2, 1, 3)
        v = jnp.einsum('btd,od->bto', x, Wv).reshape(Bx, Tx, G, HD).transpose(0, 2, 1, 3)
        q = _rms(q, q_norm_scale)
        k = _rms(k, k_norm_scale)
        pos = kv_lens[:, None] + jnp.arange(Tx, dtype=jnp.int32)
        q = _rope(q, pos)
        k = _rope(k, pos)
        slot = pos // BLOCK
        off = pos % BLOCK
        blk = jnp.take_along_axis(block_tables, slot, axis=1)
        k_blocks = k_blocks.at[blk, :, off, :].set(k.transpose(0, 2, 1, 3))
        v_blocks = v_blocks.at[blk, :, off, :].set(v.transpose(0, 2, 1, 3))
        k_all = k_blocks[block_tables].transpose(0, 2, 1, 3, 4).reshape(Bx, G, -1, HD)
        v_all = v_blocks[block_tables].transpose(0, 2, 1, 3, 4).reshape(Bx, G, -1, HD)
        S = k_all.shape[2]
        qg = q.reshape(Bx, G, GSZ, Tx, HD)
        scores = jnp.einsum('bghtd,bgsd->bghts', qg, k_all) * SCALE
        kpos = jnp.arange(S, dtype=jnp.int32)
        allowed = (kpos[None, None, :] <= pos[:, :, None]) & (kpos[None, None, :] > pos[:, :, None] - WINDOW)
        scores = jnp.where(allowed[:, None, None, :, :], scores, -jnp.inf)
        p = jax.nn.softmax(scores, axis=-1)
        o = jnp.einsum('bghts,bgsd->bghtd', p, v_all).reshape(Bx, H, Tx, HD)
        o = o.transpose(0, 2, 1, 3).reshape(Bx, Tx, H * HD)
        return jnp.einsum('bto,do->btd', o, Wo)

    def _L2_cond_ref(x, subjects, weights):
        import jax, jax.numpy as jnp
        import numpy as np
        B, C, D, T, N_SUBJECTS = (128, 32, 32, 256, 8)
        w = weights[subjects]
        out = jnp.einsum('bct,bcd->bdt', x, w)
        return out

    def _L3_cond_ref(x, subjects, weights, bias):
        import jax, jax.numpy as jnp
        import numpy as np
        B, C, T = (64, 32, 256)
        D, N = (32, 8)
        w = weights[subjects]
        b = bias[subjects]
        out = jnp.einsum('bct,bcd->bdt', x, w)
        out = out + b[:, :, None]
        return out
    x = x + _L0_cond_ref(x, itok_B_1_198, L0_cond_weights)
    x = x + _L1_cond_ref(x, L1_cond_Wq, L1_cond_Wk, L1_cond_Wv, L1_cond_Wo, L1_cond_q_norm_scale, L1_cond_k_norm_scale, L1_cond_k_blocks, L1_cond_v_blocks, itok_Bx257_0_4111, itok_B_37_3939)
    x = x + _L2_cond_ref(x, itok_B_0_7, L2_cond_weights)
    x = x + _L3_cond_ref(x, itok_B_0_7, L3_cond_weights, fside_8xS_0)
    return x

_drawn_inputs = setup_inputs


def setup_inputs(seed=0):
    import zlib

    import numpy as np

    out = dict(_drawn_inputs(seed))
    spreads = {}
    factors = {'fside_8xS_0': 3.405,
     'L1_cond_q_norm_scale': 8.0,
     'L1_cond_k_norm_scale': 64.0,
     'L1_cond_k_blocks': 3.406,
     'L1_cond_Wk': 2.989}
    for name, (base, spread) in spreads.items():
        noise = np.random.default_rng([zlib.crc32(name.encode()), seed]).standard_normal(out[name].shape)
        drawn = base * np.exp(spread * noise) if base else spread * noise
        out[name] = jnp.asarray(drawn.astype(out[name].dtype))
    for name, factor in factors.items():
        out[name] = (out[name] * factor).astype(out[name].dtype)
    return out
```

```python
import math
from contextlib import ExitStack

import numpy as np
import concourse.bass as bass
from concourse import mybir

F32 = mybir.dt.float32
I32 = mybir.dt.int32
ALU = mybir.AluOpType
ACT = mybir.ActivationFunctionType
AX = mybir.AxisListType

P = 128
B, T, D = 128, 32, 256
H, G, HD = 8, 4, 32
GSZ = H // G
BLOCK, WINDOW = 16, 128
SUBJ = 8
EPS = 1e-6
TB = P // T
NT = B // TB
SPAN = WINDOW // BLOCK
NI = 3
SLOTS = SPAN + NI
JH = (SLOTS + 1) // 2
WS = 2 * JH
GB = 8
NG = B // GB
WP = GB * WS
WPX = (2 * GB - 1) * JH + 8
KEYS = WS * BLOCK
BE = G * BLOCK * HD
FAR = 1.0e6
MASKED = -1.0e30
HEADS = H + G
QK = HEADS * HD
QKV = QK + G * HD

C_ID, C_BM, C_KAP, C_INV, C_IOTA, C_ITEM = 0, 128, 132, 132 + KEYS, 148 + KEYS, 148 + KEYS + 388
C_END = C_ITEM + NI


def constants():
    c = np.zeros((P, C_END), np.float32)
    p = np.arange(P)
    c[:, C_ID:C_ID + P] = np.eye(P)
    c[:, C_BM:C_BM + TB] = (p[:, None] // T == np.arange(TB))
    h, r, o, j = np.meshgrid(np.arange(2), np.arange(4), np.arange(4), np.arange(JH), indexing="ij")
    c[:, C_KAP:C_KAP + KEYS] = ((JH * h + j) * BLOCK + 4 * o + r).reshape(-1)
    half = HD // 2
    c[:, C_INV:C_INV + half] = np.float32(1.0) / np.float32(10000.0) ** (np.arange(half, dtype=np.float32) / np.float32(half))
    c[:, C_IOTA:C_IOTA + 388] = np.arange(388)
    c[:, C_ITEM:C_ITEM + NI] = NI * p[:, None] + np.arange(NI)
    return c


def valid(index, count):
    return not isinstance(index, int) or 0 <= index < count


def wait(eng, sem, value):
    if not isinstance(value, int) or value > 0:
        eng.wait_ge(sem, value)


def wait_first(eng, sem, value, passed):
    wait(eng, sem, value)
    if not isinstance(value, int):
        eng.sem_inc(passed, 1)


def build(nc, x, conditions, tables, kv_lens, subjects, bias, w0, w2, w3, wqkv, wo, q_scale, k_scale,
          k_cache, v_cache, consts, out):
    NBLK = tables.shape[1]
    NCACHE = k_cache.shape[0]
    ctx = ExitStack()
    with ctx:
        def sb(name, shape, dt=F32):
            return ctx.enter_context(nc.sbuf_tensor(name, shape, dt))

        def sem(name):
            return ctx.enter_context(nc.semaphore(name))

        d_w = [nc.dram_tensor(f"d_w{k}", (B, T * T), F32).ap() for k in range(3)]
        d_item = nc.dram_tensor("d_item", (B, NI), F32).ap()
        d_m1 = nc.dram_tensor("d_m1", (P, P), F32).ap()
        d_m2 = nc.dram_tensor("d_m2", (P, P), F32).ap()
        d_win = nc.dram_tensor("d_win", (2, B, WS), F32).ap()
        new_rows = nc.dram_tensor("new_rows", (B * NI * BLOCK, 2 * G * HD), F32).ap()
        patched = [nc.dram_tensor(f"patched_{k}", (B * NI, BE), F32).ap() for k in "kv"]

        xall = sb("xall", [P, NT, D])
        qt = sb("qt", [P, NT, TB, GSZ, T])
        wc = [sb(f"wc{k}", [P, NT, T]) for k in range(3)]
        wqkv_sb = sb("wqkv_sb", [P, 2, QKV])
        wo_sb = sb("wo_sb", [P, GSZ, D])
        cst = sb("cst", [P, C_END])
        gain = sb("gain", [P, HEADS, HD])
        scales = sb("scales", [P, 2, HD])
        cos = sb("cos", [P, NT, HD // 2])
        sin = sb("sin", [P, NT, HD // 2])
        t1 = sb("t1", [P, P])
        t2 = sb("t2", [P, P])
        toki = sb("toki", [P, NT], I32)
        wini = sb("wini", [P, 2, NG], I32)
        bounds = sb("bounds", [P, B // 2, 2])
        bnd = sb("bnd", [P, 4])
        rowi = sb("rowi", [P, 4], I32)
        blki = sb("blki", [P, 2, 2], I32)
        arena = sb("arena", [P, 4, 2, BE])
        stage = arena[:, 3].rearrange("p a (h o e) -> p (a h) o e", h=1, o=BLOCK // 2)
        vkeys = arena[:, 2].rearrange("p a (m e) -> p a m e", m=2 * GB)
        ktr = arena[:, 3, :, 0:WP * BLOCK]
        ktr = ktr.rearrange("p a (r m e) -> p a m r e", r=4, m=2 * GB)

        ident = cst[:, C_ID:C_ID + P]
        bmask = cst[:, C_BM:C_BM + TB]
        kappa = cst[:, C_KAP:C_KAP + KEYS]
        inv = cst[:, C_INV:C_INV + HD // 2]

        def iota(n, first=0):
            return cst[:, C_IOTA + first:C_IOTA + first + n]

        WORK = 10240
        work = sb("work", [P, WORK])
        small = sb("small", [P, 512])
        smalli = sb("smalli", [P, 16], I32)
        at = [0]

        def cut(n, dt=None):
            a = work[:, at[0]:at[0] + n]
            at[0] += n
            assert at[0] <= WORK, at[0]
            return a

        tab_f = cut(NBLK + 3)[:, 0:NBLK]
        tab_i = cut(NBLK + 3)[:, 0:NBLK].bitcast(I32)
        pick = cut(NBLK + 3)[:, 0:NBLK]
        item_row = cut(B * NI)
        same = cut(NI * B * NI).rearrange("p (s i) -> p s i", s=NI)
        later = cut(NI * B * NI).rearrange("p (s i) -> p s i", s=NI)
        repm = cut(B * NI)
        m1 = cut(P)
        m2 = cut(P)
        pack = cut(32 + 32 + 64 + 64 + 2 * WS)
        p_tok, p_pos = pack[:, 0:32], pack[:, 32:64]
        p_up = pack[:, 64:128].rearrange("p (h t) -> p h t", h=GSZ)
        p_low = pack[:, 128:192].rearrange("p (h t) -> p h t", h=GSZ)
        p_win = pack[:, 192:192 + 2 * WS].rearrange("p (k j) -> p k j", k=2)
        ang = cut(NT * (HD // 2)).rearrange("p (n d) -> p n d", n=NT)
        turn = cut(NT * (HD // 2)).rearrange("p (n d) -> p n d", n=NT)
        biasg = cut(T)
        at[0] = 0
        wbd = [cut(P) for _ in range(2)]
        x1s = [cut(D) for _ in range(2)]
        x1t = [cut(D).rearrange("p (c t) -> p c t", c=2) for _ in range(2)]
        sq = [cut(QK) for _ in range(2)]
        qn = [cut(QK) for _ in range(2)]
        qg = [cut(QK) for _ in range(2)]
        ra = [cut(QK) for _ in range(2)]
        rb = [cut(QK) for _ in range(2)]
        qkvr = [cut(QKV) for _ in range(4)]
        st = [cut(3 * HEADS) for _ in range(2)]
        at[0] = 0
        qs = [cut(GB * GSZ * T) for _ in range(2)]
        msk = [cut(2 * KEYS) for _ in range(2)]
        mska, mskb = (cut(2 * KEYS).rearrange("p (q k) -> p q k", q=2) for _ in range(2))
        smx = [cut(2 * KEYS).rearrange("p (q k) -> p q k", q=2) for _ in range(2)]
        prob = [cut(4 * P).rearrange("p (q h k) -> p q h k", q=2, h=2) for _ in range(2)]
        pts = [cut(4 * P).rearrange("p (g k) -> p g k", g=4) for _ in range(2)]
        on = [cut(2 * P) for _ in range(2)]
        ot = [cut(GSZ * P).rearrange("p (h b t) -> p h b t", h=GSZ, b=TB) for _ in range(2)]
        wbd2 = [cut(P) for _ in range(2)]
        wbd3 = [cut(P) for _ in range(2)]
        x2 = [cut(D) for _ in range(2)]
        x3 = [cut(D) for _ in range(2)]
        x4 = [cut(D) for _ in range(2)]
        ka = cut(G * 4 * WP).rearrange("p (g k) -> p g k", g=G)
        nmax = [cut(2) for _ in range(2)]
        rsum = [cut(2 * G) for _ in range(2)]
        rinv = [cut(2 * G) for _ in range(2)]

        kv_i, f_i, s_i, sub_i, con_i = (smalli[:, k:k + 1] for k in range(5))
        blk_i = smalli[:, 8:8 + NI]
        kv_f, f_f, s_f, f32_f, low_f = (small[:, k:k + 1] for k in range(5))
        eps_c = small[:, 5:6]
        sidx = small[:, 8:8 + SLOTS]
        blk = small[:, 24:24 + SLOTS]
        rep = small[:, 40:40 + SLOTS]
        hit = small[:, 56:56 + SLOTS]
        base = small[:, 72:72 + NI]
        fmask = small[:, 80:96]
        cov = small[:, 96:144]
        wins = small[:, 144:192]
        keep = small[:, 192:240]
        cell = small[:, 240:288]
        ft = small[:, 288:320]
        tmp48 = small[:, 320:368]
        miss = small[:, 368:368 + SLOTS]

        ps = [ctx.enter_context(nc.psum_tensor(f"ps{k}", [P, 512], F32)) for k in range(8)]

        s_kv, s_tab, s_cs, s_idx, s_cst = sem("kv_loaded"), sem("tables_loaded"), sem("choices_loaded"), sem("items_stored"), sem("consts_loaded")
        s_x, s_wts, s_scl = sem("x_loaded"), sem("weights_loaded"), sem("scales_loaded")
        s_mixg, s_mixd, s_mix = sem("mixes_gathered"), sem("mixes_stored"), sem("mixes_loaded")
        s_itemrow, s_blk, s_blki = sem("item_row_loaded"), sem("blocks_found"), sem("block_indices")
        s_itemg = sem("item_blocks_gathered")
        s_zero, s_zeroed = sem("zero_tile"), sem("new_rows_zeroed")
        s_pairs, s_cnt = sem("item_pairs"), sem("later_counts")
        s_pack, s_packd, s_m = sem("pack_ready"), sem("pack_stored"), sem("matrices_loaded")
        s_mz, s_mt, s_tidx = sem("matrix_cleared"), sem("matrices_transposed"), sem("indices_ready")
        s_trig, s_red = sem("angles_done"), sem("angles_reduced")
        s_dve = sem("vector_step")
        s_gain, s_masked = sem("gain_ready"), sem("old_rows_masked")
        s_pre = sem("prelude_done")
        s_wbd, s_l0, s_x1, s_xc, s_xt, s_xtc, s_qkv = (sem(n) for n in ("mix0_ready", "mix0_done", "x1_ready", "x1_kept", "x1_transposed", "x1t_ready", "qkv_done"))
        s_sq, s_v, s_ss, s_st, s_rc, s_qn, s_qg, s_ra, s_rb, s_qr, s_qt, s_qtc = (sem(n) for n in (
            "squares", "v_copied", "square_sums", "norms", "norm_recips", "normed", "gained", "rope_cos", "rope_sin",
            "qk_ready", "q_transposed", "qt_ready"))
        s_scat = [sem(f"rows_scattered{k}") for k in range(4)]
        s_stage = [sem(f"new_rows_loaded{k}") for k in range(2)]
        s_addk, s_addv, s_patched = sem("k_patched"), sem("v_patched"), sem("patched_stored")
        s_old = [sem(f"old_blocks_loaded{k}") for k in range(2)]
        s_win = [sem(f"window_loaded{k}") for k in range(2)]
        s_kvt, s_kc, s_vc, s_qs = sem("window_transposed"), sem("keys_ready"), sem("values_ready"), sem("queries_staged")
        s_kd = [sem(f"keys_moved{k}") for k in range(2)]
        s_bd = sem("bounds_staged")
        s_passed = [sem("gpsimd_passed"), sem("sync_passed")]
        s_ma, s_mk = sem("mask_parts"), sem("mask_ready")
        s_s, s_sm, s_nm, s_e, s_pt, s_pv = (sem(n) for n in (
            "scores", "masked_scores", "row_max", "probs", "probs_transposed", "pv_done"))
        s_rl, s_on, s_ot, s_oc, s_wo, s_w23 = (sem(n) for n in ("sum_recips", "o_normed", "o_transposed", "ot_ready", "wo_done", "mix23_ready"))
        s_x2, s_l2, s_x3, s_l3, s_x4 = (sem(n) for n in ("x2_ready", "mix2_done", "x3_ready", "mix3_done", "x4_ready"))
        s_out = [sem(f"out_stored{k}") for k in range(2)]
        s_pc = [sem(f"probs_t_ready{k}") for k in range(2)]
        s_pz, s_ri, s_bi = sem("probs_cleared"), sem("row_indices"), sem("window_indices")

        psl, psx, psq, psqt = ps[0:2], ps[2:4], ps[4:6], ps[6:8]
        pss, pspt, pskv = ps[0:2], ps[2:4], ps[4:6]
        pso, psot = ps[6][:, 0:256], ps[7][:, 0:256]
        psw = [ps[7][:, 256:512], ps[7][:, 0:256]]

        xv = x.rearrange("(n b) c t -> (b c) n t", b=TB)
        outv = out.rearrange("(n b) c t -> n (b c) t", b=TB)
        mixv = [d.rearrange("(n b) (c d) -> (b c) n d", b=TB, c=T) for d in d_w]
        rowsv = new_rows.rearrange("(b s o) e -> s b o e", s=NI, o=BLOCK)
        patchedv = [d.rearrange("(b s) e -> s b e", s=NI) for d in patched]
        cachev = [c.rearrange("n g o d -> n (g o d)") for c in (k_cache, v_cache)]

        A_UN = 4
        NU = NG * GB

        block = ctx.enter_context(nc.Block())

        def store_item(sp, s):
            sp.wait_ge(s_addk, 2 * s + 2)
            sp.wait_ge(s_addv, 2 * s + 2)
            for k in range(2):
                sp.dma_start(patchedv[k][s], arena[:, s, k]).then_inc(s_patched, 16)

        def xmix(k):
            q = qt[:, :, :, :, :].rearrange("p n b h t -> p (n b h t)")
            return q[:, k * T * T:(k + 1) * T * T]

        def run_b(eng, slot):
            for i in (-1, 0):
                for c in range(16):
                    slot(i, c)
            with eng.Fori(1, NG // 2 - 1) as i:
                for c in range(16):
                    slot(i, c)
            for i in (NG // 2 - 1, NG // 2):
                for c in range(16):
                    slot(i, c)

        def ktr_rows(par, g, r):
            return arena[HD * g:HD * (g + 1), 3, par, 4 * WP * r:4 * WP * (r + 1)]

        def window_columns(bank):
            a = bank[:, 0:4 * WPX].rearrange("p (o m) -> p o m", o=4)
            lap = a[:, :, 0:8].unsqueeze(1).broadcast_to([P, 2 * GB, 4, 8])
            return bass.AP(tensor=lap.tensor, offset=lap.offset, ap=[lap.ap[0], [JH, 2 * GB], lap.ap[2], lap.ap[3]])

        @block.sync
        def _(sp):
            sp.dma_start(kv_i, kv_lens.unsqueeze(1)).then_inc(s_kv, 16)
            sp.dma_start(sub_i, subjects.unsqueeze(1)).then_inc(s_cs, 16)
            sp.dma_start(con_i, conditions.unsqueeze(1)).then_inc(s_cs, 16)
            sp.dma_start(cst[:, :], consts).then_inc(s_cst, 16)
            sp.dma_start(tab_i, tables).then_inc(s_tab, 16)
            sp.dma_start(scales[:, 0], q_scale.partition_broadcast(P)).then_inc(s_scl, 16)
            sp.dma_start(scales[:, 1], k_scale.partition_broadcast(P)).then_inc(s_scl, 16)
            sp.dma_start(xall[:, :, :], xv).then_inc(s_x, 16)
            sp.dma_start(wqkv_sb[:, :, :], wqkv).then_inc(s_wts, 16)
            sp.dma_start(wo_sb[:, :, :], wo).then_inc(s_wts, 16)
            sp.wait_ge(s_blk, 1)
            sp.dma_start(d_item, blk[:, SPAN:SLOTS]).then_inc(s_idx, 16)
            sp.wait_ge(s_mixg, 64)
            for k in range(3):
                sp.dma_start(d_w[k], xmix(k)).then_inc(s_mixd, 16)
            sp.dma_start(d_m2[96:128, :].rearrange("n (b t) -> (n b) t", b=TB), biasg).then_inc(s_mixd, 16)
            sp.wait_ge(s_idx, 16)
            sp.dma_start(item_row, d_item.rearrange("b s -> (b s)").partition_broadcast(P)).then_inc(s_itemrow, 16)
            sp.wait_ge(s_mixd, 64)
            for k in range(3):
                sp.dma_start(wc[k][:, :, :], mixv[k]).then_inc(s_mix, 16)
            sp.wait_ge(s_zero, 1)
            for s in range(NI):
                sp.dma_start(rowsv[s], arena[:, 3].rearrange("p a e -> p (a e)")
                             .rearrange("p (o e) -> p o e", o=BLOCK)).then_inc(s_zeroed, 16)
            sp.wait_ge(s_pack, 1)
            sp.dma_start(d_m1[0:32, :].rearrange("n (b t) -> (n b) t", b=TB), p_tok).then_inc(s_packd, 16)
            sp.dma_start(d_m1[32:64, :].rearrange("n (b t) -> (n b) t", b=TB), p_pos).then_inc(s_packd, 16)
            sp.dma_start(d_m1[64:128, :].rearrange("n (b t) -> (n b) t", b=2), pack[:, 64:128]).then_inc(s_packd, 16)
            sp.dma_start(d_m2[0:64, :].rearrange("n (b t) -> (n b) t", b=2), pack[:, 128:192]).then_inc(s_packd, 16)
            for k in range(2):
                sp.dma_start(d_win[k], p_win[:, k]).then_inc(s_packd, 16)
            sp.wait_ge(s_packd, 96)
            sp.wait_ge(s_mz, 1)
            sp.dma_start(m1, d_m1).then_inc(s_m, 16)
            sp.dma_start(m2[0:64, :], d_m2[0:64, :]).then_inc(s_m, 16)
            sp.dma_start(m2[96:128, :], d_m2[96:128, :]).then_inc(s_m, 16)
            for k in range(2):
                sp.dma_start(m2[64 + NG * k:64 + NG * (k + 1), 0:WP],
                             d_win[k].rearrange("(n b) j -> n (b j)", b=GB)).then_inc(s_m, 16)
            for k in range(4):
                sp.wait_ge(s_scat[k], 16 * (NT // 4))
            sp.wait_ge(s_zeroed, 48)
            for w in range(2 * NI):
                s, h = w // 2, w % 2
                if w >= 2:
                    sp.wait_ge(s_addk, w - 1)
                    sp.wait_ge(s_addv, w - 1)
                sp.dma_start(stage[:, w % 2], rowsv[s][:, 8 * h:8 * h + 8, :]).then_inc(s_stage[w % 2], 16)
                if w >= 3 and w % 2:
                    store_item(sp, (w - 3) // 2)
            store_item(sp, NI - 1)
            def b_slot(i, c):
                w = c % GB - 1
                g, par = 2 * i + c // GB + 1, (c // GB + 1) % 2
                if valid(g, NG) and 0 <= w < G:
                    wait_first(sp, s_kc, 4 * g + w + 1, s_passed[1])
                    wait(sp, s_s, GB * (g - 1))
                    for r in range(4):
                        sp.dma_start(ktr_rows(par, w, r), ka[HD * r:HD * (r + 1), w]).then_inc(s_kd[par], 16)
                if c % 4 == 1:
                    n, b = 4 * i + (c - 9) // 4, ((c - 9) // 4) % 2
                    if valid(n, NT):
                        wait_first(sp, s_x4, n + 1, s_passed[1])
                        sp.dma_start(outv[n], x4[b]).then_inc(s_out[b], 16)
            run_b(sp, b_slot)
            for k in range(2):
                sp.wait_ge(s_out[k], 16 * (NT // 2))

        @block.gpsimd
        def _(pool):
            pool.memset(arena[:, 3], 0.0).then_inc(s_zero, 1)
            pool.memset(m2, 0.0).then_inc(s_mz, 1)
            pool.wait_ge(s_cs, 32)
            for k, (w, i, n) in enumerate(((w0, con_i, w0.shape[0]), (w2, sub_i, SUBJ), (w3, sub_i, SUBJ))):
                pool.indirect_dma_start(out=xmix(k), out_offset=None, in_=w.rearrange("n c d -> n (c d)"),
                                        in_offset=bass.IndirectOffsetOnAxis(ap=i, axis=0),
                                        bounds_check=n - 1, oob_is_err=False).then_inc(s_mixg, 16)
            pool.indirect_dma_start(out=biasg, out_offset=None, in_=bias,
                                    in_offset=bass.IndirectOffsetOnAxis(ap=sub_i, axis=0),
                                    bounds_check=SUBJ - 1, oob_is_err=False).then_inc(s_mixg, 16)
            pool.wait_ge(s_blki, 1)
            for s in range(NI):
                for k in range(2):
                    pool.indirect_dma_start(out=arena[:, s, k], out_offset=None, in_=cachev[k],
                                            in_offset=bass.IndirectOffsetOnAxis(ap=blk_i[:, s:s + 1], axis=0),
                                            bounds_check=NCACHE - 1, oob_is_err=False).then_inc(s_itemg, 16)
            pool.wait_ge(s_mix, 48)
            pool.wait_ge(s_gain, 1)

            def expand(dst, src, sm):
                nc.gpsimd.tensor_tensor(dst.rearrange("p (b d) -> p b d", b=TB),
                                        src.unsqueeze(1).broadcast_to([P, TB, T]),
                                        bmask.unsqueeze(2).broadcast_to([P, TB, T]), ALU.mult).then_inc(sm, 1)

            def a_slot(i, c):
                k = A_UN * i + c - 4
                if valid(k, NT):
                    b = (c - 4) % 2
                    pool.wait_ge(s_qn, k + 1)
                    wait(pool, s_rb, 2 * k - 2)
                    wait(pool, s_ra, k - 1)
                    nc.gpsimd.tensor_tensor(qg[b], qn[b], gain[:, :, :].rearrange("p h d -> p (h d)"), ALU.mult).then_inc(s_qg, 1)
                    pool.wait_ge(s_qg, k + 1)
                    wait(pool, s_qr, 2 * k - 2)
                    nc.gpsimd.tensor_tensor(ra[b].rearrange("p (h d) -> p h d", d=HD // 2),
                                            qg[b].rearrange("p (h d) -> p h d", d=HD // 2),
                                            cos[:, k, :].unsqueeze(1).broadcast_to([P, 2 * HEADS, HD // 2]),
                                            ALU.mult).then_inc(s_ra, 1)
                k = A_UN * i + c + 1
                if valid(k, NT):
                    wait(pool, s_l0, k - 1)
                    expand(wbd[(c + 1) % 2], wc[0][:, k, :], s_wbd)
                k = A_UN * i + c - 5
                if valid(k, NT):
                    r = (c - 5) % 4
                    pool.wait_ge(s_qr, 2 * k + 2)
                    pool.wait_ge(s_v, k + 1)
                    wait(pool, s_scat[r], 16 * (i + (c - 9) // 4 + 1))
                    nc.gpsimd.tensor_copy(rowi[:, r:r + 1], toki[:, bass.ds(k, 1)]).then_inc(s_ri, 1)
                    wait_first(pool, s_ri, k + 1, s_passed[0])
                    pool.indirect_dma_start(out=new_rows,
                                            out_offset=bass.IndirectOffsetOnAxis(ap=rowi[:, r:r + 1], axis=0),
                                            in_=qkvr[r][:, H * HD:QKV], in_offset=None,
                                            bounds_check=B * NI * BLOCK - 1, oob_is_err=False).then_inc(s_scat[r], 16)

            pool.wait_ge(s_pre, 1)
            expand(wbd[0], wc[0][:, 0, :], s_wbd)
            pool.wait_ge(s_zeroed, 48)
            pool.wait_ge(s_trig, 2)
            for n in range(3 * A_UN):
                a_slot(n // A_UN, n % A_UN)
            with pool.Fori(3, NT // A_UN - 1) as i:
                for c in range(A_UN):
                    a_slot(i, c)
            for n in range(NT - A_UN, NT + 6):
                a_slot(n // A_UN, n % A_UN)

            for w in range(2 * NI):
                s, h = w // 2, w % 2
                pool.wait_ge(s_stage[w % 2], 16 * (w // 2 + 1))
                pool.wait_ge(s_masked, 2 * NI)
                o = arena[:, s, 1].rearrange("p (g o d) -> p g o d", g=G, o=BLOCK)[:, :, 8 * h:8 * h + 8, :]
                nc.gpsimd.tensor_tensor(o, o, stage[:, w % 2, :, G * HD:2 * G * HD]
                                        .rearrange("p o (g d) -> p g o d", g=G), ALU.add).then_inc(s_addv, 1)

            def b_slot(i, c):
                if c % GB == 0:
                    g, par = 2 * i + c // GB + 2, (c // GB) % 2
                    if valid(g, NG):
                        if isinstance(g, int) and g < 2:
                            pool.wait_ge(s_patched, 32 * NI)
                        wait(pool, s_kvt, GB * (g - 1))
                        wait(pool, s_win[par], 32 * (i + 1))
                        nc.gpsimd.tensor_copy(blki[0:WP, par], wini[0:WP, :, bass.ds(g, 1)].rearrange("p k a -> p (k a)")).then_inc(s_bi, 1)
                        wait_first(pool, s_bi, g + 1, s_passed[0])
                        for k in range(2):
                            pool.indirect_dma_start(out=arena[0:WP, par, k], out_offset=None, in_=cachev[k],
                                                    in_offset=bass.IndirectOffsetOnAxis(ap=blki[0:WP, par, 0:1], axis=0),
                                                    bounds_check=NCACHE - 1, oob_is_err=False).then_inc(s_old[par], 16)
                if c % GB == 2:
                    g, par = 2 * i + c // GB + 2, (c // GB) % 2
                    if valid(g, NG):
                        wait_first(pool, s_old[par], 32 * (i + 2), s_passed[0])
                        for k in range(2):
                            pool.indirect_dma_start(out=arena[0:WP, par, k], out_offset=None, in_=patched[k],
                                                    in_offset=bass.IndirectOffsetOnAxis(ap=blki[0:WP, par, 1:2], axis=0),
                                                    bounds_check=B * NI - 1, oob_is_err=False).then_inc(s_win[par], 16)
                if c % GB == 1:
                    g, par = 2 * i + c // GB + 1, (c // GB + 1) % 2
                    if valid(g, NG):
                        wait(pool, s_s, GB * (g - 1))
                        if isinstance(g, int) and g == 0:
                            pool.wait_ge(s_qtc, NT)
                        nc.gpsimd.tensor_copy(qs[par], qt[:, bass.ds(2 * g, 2)].rearrange("p n b h t -> p (n b h t)")).then_inc(s_qs, 1)
                if c % 4 == 2:
                    n, par = 4 * i + c // 4 + 1, (c // 4 + 1) % 2
                    if valid(n, NT):
                        wait(pool, s_mk, n)
                        nc.gpsimd.tensor_copy(bnd[:, :], bounds[:, bass.ds(2 * n, 2), :].rearrange("p a k -> p (a k)")).then_inc(s_bd, 1)
                        wait_first(pool, s_bd, n + 1, s_passed[0])
                        for q in range(2):
                            nc.gpsimd.tensor_scalar(mska[:, q], kappa, bnd[:, 2 * q:2 * q + 1], None, ALU.is_gt).then_inc(s_ma, 1)
                            nc.gpsimd.tensor_scalar(mskb[:, q], kappa, bnd[:, 2 * q + 1:2 * q + 2], None, ALU.is_le).then_inc(s_ma, 1)
                        wait(pool, s_sm, 4 * n - 4)
                        pool.wait_ge(s_ma, 4 * n + 4)
                        nc.gpsimd.tensor_tensor(msk[par], mska.rearrange("p q k -> p (q k)"),
                                                mskb.rearrange("p q k -> p (q k)"), ALU.add).then_inc(s_mk, 1)
                if c % 4 == 0:
                    n, par = 4 * i + c // 4 - 1, (c // 4 - 1) % 2
                    if valid(n, NT):
                        wait(pool, s_l2, n - 1)
                        wait(pool, s_l3, n - 1)
                        expand(wbd2[par], wc[1][:, bass.ds(n, 1), :].rearrange("p a d -> p (a d)"), s_w23)
                        expand(wbd3[par], wc[2][:, bass.ds(n, 1), :].rearrange("p a d -> p (a d)"), s_w23)

            pool.wait_ge(s_qtc, NT)
            for b in range(2):
                nc.gpsimd.memset(prob[b].rearrange("p g h k -> p (g h k)"), 0.0).then_inc(s_pz, 1)
            run_b(pool, b_slot)

        @block.vector
        def _(dve):
            v = nc.vector
            steps = [0]

            def link(ins):
                steps[0] += 1
                ins.then_inc(s_dve, 1)
                dve.wait_ge(s_dve, steps[0])

            dve.wait_ge(s_kv, 16)
            dve.wait_ge(s_cst, 16)
            v.tensor_scalar(f_i, kv_i, BLOCK - 1, None, ALU.bitwise_and)
            link(v.tensor_scalar(s_i, kv_i, int(math.log2(BLOCK)), None, ALU.arith_shift_right))
            v.tensor_copy(kv_f, kv_i)
            v.tensor_copy(f_f, f_i)
            link(v.tensor_copy(s_f, s_i))
            link(v.tensor_scalar(sidx, iota(SLOTS), s_f, float(-SPAN), ALU.add, ALU.add))
            link(v.tensor_scalar(sidx, sidx, 0.0, float(NBLK - 1), ALU.max, ALU.min))
            dve.wait_ge(s_tab, 16)
            link(v.tensor_copy(tab_f, tab_i))
            for j in range(SLOTS):
                link(v.scalar_tensor_tensor(pick, iota(NBLK), sidx[:, j:j + 1], tab_f, ALU.is_equal, ALU.mult,
                                            accum_out=blk[:, j:j + 1]))
            link(v.tensor_copy(blk_i, blk[:, SPAN:SLOTS]))
            v.sem_inc(s_blk, 1)
            v.sem_inc(s_blki, 1)
            link(v.tensor_scalar(f32_f, f_f, float(T), None, ALU.add))
            link(v.tensor_scalar(tmp48, iota(NI * BLOCK), f_f, None, ALU.is_ge))
            link(v.scalar_tensor_tensor(cov, iota(NI * BLOCK), f32_f, tmp48, ALU.is_lt, ALU.mult))
            dve.wait_ge(s_itemrow, 16)
            for s in range(NI):
                link(v.tensor_scalar(same[:, s], item_row, blk[:, SPAN + s:SPAN + s + 1], None, ALU.is_equal))
                link(v.scalar_tensor_tensor(later[:, s], iota(B * NI), cst[:, C_ITEM + s:C_ITEM + s + 1], same[:, s],
                                            ALU.is_lt, ALU.mult))
            v.sem_inc(s_pairs, 1)
            for j in range(SLOTS):
                link(v.scalar_tensor_tensor(repm, item_row, blk[:, j:j + 1], iota(B * NI, 1), ALU.is_equal, ALU.mult))
                link(v.tensor_reduce(rep[:, j:j + 1], repm, AX.X, ALU.max))
            v.tensor_scalar(p_pos, iota(T), kv_f, None, ALU.add)
            link(v.tensor_scalar(ft, iota(T), f_f, None, ALU.add))
            link(v.tensor_scalar(low_f, s_f, float(-BLOCK), float(WINDOW - 1), ALU.mult, ALU.add))
            for h in range(GSZ):
                v.tensor_scalar(p_up[:, h], ft, float(WINDOW), None, ALU.add)
                v.tensor_scalar(p_low[:, h], ft, low_f, None, ALU.max)
            link(v.memset(p_win[:, 0], FAR))
            link(v.memset(p_win[:, 1], FAR))
            link(v.tensor_scalar(hit, rep, 0.0, None, ALU.is_gt))
            link(v.tensor_scalar(miss, rep, 0.0, None, ALU.is_equal))
            link(v.scalar_tensor_tensor(p_win[:, 0, 0:SLOTS], hit, FAR, blk, ALU.mult, ALU.add))
            link(v.scalar_tensor_tensor(miss, miss, FAR, rep, ALU.mult, ALU.add))
            link(v.tensor_scalar(p_win[:, 1, 0:SLOTS], miss, -1.0, None, ALU.add))
            dve.wait_ge(s_cnt, 1)
            link(v.scalar_tensor_tensor(wins, ps[0][:, 0:48], 0.0, cov, ALU.is_equal, ALU.mult))
            link(v.tensor_scalar(keep, ps[1][:, 0:48], 0.0, None, ALU.is_equal))
            link(v.tensor_scalar(base, rep[:, SPAN:SLOTS], float(BLOCK), -float(BLOCK) - FAR, ALU.mult, ALU.add))
            for s in range(NI):
                v.scalar_tensor_tensor(cell[:, 16 * s:16 * s + 16], iota(BLOCK), base[:, s:s + 1],
                                       wins[:, 16 * s:16 * s + 16], ALU.add, ALU.mult)
            link(v.tensor_scalar(fmask, iota(BLOCK), f_f, None, ALU.is_equal))
            link(v.tensor_scalar(cell, cell, FAR, None, ALU.add))
            link(v.tensor_scalar(p_tok, cell[:, 0:T], fmask[:, 0:1], None, ALU.mult))
            for f in range(1, BLOCK):
                link(v.scalar_tensor_tensor(p_tok, cell[:, f:f + T], fmask[:, f:f + 1], p_tok, ALU.mult, ALU.add))
            v.sem_inc(s_pack, 1)
            dve.wait_ge(s_scl, 32)
            link(v.tensor_scalar(gain[:, 0:H, :], scales[:, 0].unsqueeze(1).broadcast_to([P, H, HD]),
                                 1.0, 256.0 ** -0.5, ALU.add, ALU.mult))
            link(v.tensor_scalar(gain[:, H:HEADS, :], scales[:, 1].unsqueeze(1).broadcast_to([P, G, HD]),
                                 1.0, None, ALU.add))
            v.sem_inc(s_gain, 1)
            dve.wait_ge(s_mt, 1)
            v.tensor_copy(t1[:, :], ps[2][:, 0:P])
            link(v.tensor_copy(t2[:, :], ps[3][:, 0:P]))
            v.tensor_copy(toki[:, :], t1[:, 0:NT])
            v.tensor_copy(bounds[:, :, 0], t1[:, 64:128])
            v.tensor_copy(bounds[:, :, 1], t2[:, 0:64])
            link(v.tensor_copy(wini[:, :, :].rearrange("p k n -> p (k n)"), t2[:, 64:64 + 2 * NG]))
            v.sem_inc(s_tidx, 1)
            link(v.tensor_tensor(ang, t1[:, NT:2 * NT].unsqueeze(2).broadcast_to([P, NT, HD // 2]),
                                 inv.unsqueeze(1).broadcast_to([P, NT, HD // 2]), ALU.mult))
            magic = 1.5 * 2.0 ** 23
            c1 = 6.28125
            c2 = float(np.float32(math.floor((2 * math.pi - c1) * 2.0 ** 21) / 2.0 ** 21))
            c3 = float(np.float32(2 * math.pi - c1 - c2))
            link(v.tensor_scalar(turn, ang, 1.0 / (2 * math.pi), magic, ALU.mult, ALU.add))
            link(v.tensor_scalar(turn, turn, magic, None, ALU.subtract))
            for cc in (c1, c2, c3):
                link(v.scalar_tensor_tensor(ang, turn, -cc, ang, ALU.mult, ALU.add))
            lim = 3.1415925
            link(v.tensor_scalar(ang, ang, -lim, lim, ALU.max, ALU.min))
            link(v.scalar_tensor_tensor(turn, ang, -1.0, ang, ALU.mult, ALU.max))
            link(v.tensor_scalar(turn, turn, -1.0, math.pi / 2, ALU.mult, ALU.add))
            v.sem_inc(s_red, 1)
            link(v.memset(eps_c, EPS))
            dve.wait_ge(s_itemg, 32 * NI)
            for s in range(NI):
                for k in range(2):
                    o = arena[:, s, k].rearrange("p (g o d) -> p g o d", g=G, o=BLOCK)
                    m = keep[:, 16 * s:16 * s + 16].unsqueeze(1).broadcast_to([P, G, BLOCK])
                    v.tensor_tensor(o, o, m.unsqueeze(3).broadcast_to([P, G, BLOCK, HD]), ALU.mult).then_inc(s_masked, 1)
            dve.wait_ge(s_trig, 2)
            dve.wait_ge(s_masked, 2 * NI)
            v.sem_inc(s_pre, 1)

            dve.wait_ge(s_x, 16)

            def a_slot(i, c):
                k = A_UN * i + c
                if valid(k, NT):
                    dve.wait_ge(s_l0, k + 1)
                    wait(dve, s_xt, k - 1)
                    wait(dve, s_xc, k - 1)
                    v.tensor_tensor(x1s[c % 2], psl[c % 2][:, 0:D], xall[:, k, :], ALU.add).then_inc(s_x1, 1)
                k = A_UN * i + c - 3
                b = (c - 3) % 2
                if valid(k, NT):
                    dve.wait_ge(s_sq, k + 1)
                    v.tensor_reduce(st[b][:, 0:HEADS], sq[b].rearrange("p (h d) -> p h d", d=HD), AX.X, ALU.add).then_inc(s_ss, 1)
                k = A_UN * i + c - 4
                b, r = (c - 4) % 2, (c - 4) % 4
                if valid(k, NT):
                    q4 = qg[b].rearrange("p (h e d) -> p h e d", e=2, d=HD // 2)
                    b4 = rb[b].rearrange("p (h e d) -> p h e d", e=2, d=HD // 2)
                    a4 = ra[b].rearrange("p (h e d) -> p h e d", e=2, d=HD // 2)
                    o4 = qkvr[r][:, 0:QK].rearrange("p (h e d) -> p h e d", e=2, d=HD // 2)
                    sn = sin[:, k, :].unsqueeze(1).broadcast_to([P, HEADS, HD // 2])
                    dve.wait_ge(s_qg, k + 1)
                    wait(dve, s_qr, 2 * k - 2)
                    for e in range(2):
                        v.tensor_tensor(b4[:, :, e], q4[:, :, 1 - e], sn, ALU.mult).then_inc(s_rb, 1)
                    dve.wait_ge(s_rb, 2 * k + 2)
                    dve.wait_ge(s_ra, k + 1)
                    wait(dve, s_scat[r], 16 * (i + (c - 8) // 4 + 1))
                    wait(dve, s_qt, k - 3)
                    v.tensor_tensor(o4[:, :, 0], a4[:, :, 0], b4[:, :, 0], ALU.subtract).then_inc(s_qr, 1)
                    v.tensor_tensor(o4[:, :, 1], a4[:, :, 1], b4[:, :, 1], ALU.add).then_inc(s_qr, 1)
                k = A_UN * i + c - 3
                b = (c - 3) % 2
                if valid(k, NT):
                    dve.wait_ge(s_st, k + 1)
                    v.reciprocal(st[b][:, 2 * HEADS:3 * HEADS], st[b][:, HEADS:2 * HEADS]).then_inc(s_rc, 1)
                    dve.wait_ge(s_rc, k + 1)
                    wait(dve, s_qg, k - 1)
                    v.tensor_tensor(qn[b].rearrange("p (h d) -> p h d", d=HD),
                                    psq[b][:, 0:QK].rearrange("p (h d) -> p h d", d=HD),
                                    st[b][:, 2 * HEADS:3 * HEADS].unsqueeze(2).broadcast_to([P, HEADS, HD]),
                                    ALU.mult).then_inc(s_qn, 1)

            for n in range(3 * A_UN):
                a_slot(n // A_UN, n % A_UN)
            with dve.Fori(3, NT // A_UN - 1) as i:
                for c in range(A_UN):
                    a_slot(i, c)
            for n in range(NT - A_UN, NT + 6):
                a_slot(n // A_UN, n % A_UN)

            for w in range(2 * NI):
                s, h = w // 2, w % 2
                dve.wait_ge(s_stage[w % 2], 16 * (w // 2 + 1))
                o = arena[:, s, 0].rearrange("p (g o d) -> p g o d", g=G, o=BLOCK)[:, :, 8 * h:8 * h + 8, :]
                v.tensor_tensor(o, o, stage[:, w % 2, :, 0:G * HD].rearrange("p o (g d) -> p g o d", g=G),
                                ALU.add).then_inc(s_addk, 1)

            def b_slot(i, c):
                U = 16 * i + c + 1
                b = (c + 1) % 2
                if valid(U, NU):
                    dve.wait_ge(s_s, U + 1)
                    dve.wait_ge(s_mk, 4 * i + (c + 1) // 4 + 1)
                    wait(dve, s_e, U - 1)
                    v.scalar_tensor_tensor(smx[b].rearrange("p q k -> p (q k)"), msk[((c + 1) // 4) % 2], MASKED,
                                           pss[b][:, 0:2 * KEYS], ALU.mult, ALU.add).then_inc(s_sm, 1)
                    dve.wait_ge(s_sm, U + 1)
                    v.tensor_reduce(nmax[b], smx[b], AX.X, ALU.max, negate=True).then_inc(s_nm, 1)
                w = c % GB
                g, par = 2 * i + c // GB + 1, (c // GB + 1) % 2
                if valid(g, NG) and w >= 4:
                    dve.wait_ge(s_kvt, GB * g + w + 1)
                    wait(dve, s_pv, GB * (g - 1))
                    v.transpose(vkeys[:, par, :, HD * (w - 4):HD * (w - 3)], window_columns(pskv[w % 2])).then_inc(s_vc, 1)
                U = 16 * i + c
                b = c % 2
                if valid(U, NU) and b == 0:
                    dve.wait_ge(s_pt, U + 1)
                    wait(dve, s_pv, U - 1)
                    v.tensor_copy(pts[b].rearrange("p g k -> p (g k)"), pspt[b][:, :]).then_inc(s_pc[0], 1)
                if c % 4 == 0:
                    n, b = 4 * i + c // 4 - 1, (c // 4 - 1) % 2
                    if valid(n, NT):
                        dve.wait_ge(s_e, 4 * n + 4)
                        v.reciprocal(rinv[b], rsum[b]).then_inc(s_rl, 1)
                        dve.wait_ge(s_pv, 4 * n + 4)
                        dve.wait_ge(s_rl, n + 1)
                        wait(dve, s_ot, n - 1)
                        v.tensor_tensor(on[b].rearrange("p (g d) -> p g d", g=2 * G), pso.rearrange("p (g d) -> p g d", g=2 * G),
                                        rinv[b].unsqueeze(2).broadcast_to([P, 2 * G, HD]), ALU.mult).then_inc(s_on, 1)
                if c % 4 == 2:
                    n, b = 4 * i + (c - 6) // 4, ((c - 6) // 4) % 2
                    if valid(n, NT):
                        dve.wait_ge(s_wo, n + 1)
                        wait(dve, s_x3, n - 1)
                        wait(dve, s_l2, n - 1)
                        v.tensor_tensor(x2[b], psw[0], xall[:, bass.ds(n, 1), :].rearrange("p a d -> p (a d)"), ALU.add).then_inc(s_x2, 1)
                if c % 4 == 3:
                    n, b = 4 * i + (c - 7) // 4, ((c - 7) // 4) % 2
                    if valid(n, NT):
                        dve.wait_ge(s_l2, n + 1)
                        wait(dve, s_x4, n - 1)
                        wait(dve, s_l3, n - 1)
                        v.tensor_tensor(x3[b], psw[1], x2[b], ALU.add).then_inc(s_x3, 1)
                if c % 4 == 0:
                    n, b = 4 * i + (c - 8) // 4, ((c - 8) // 4) % 2
                    if valid(n, NT):
                        dve.wait_ge(s_l3, n + 1)
                        wait(dve, s_out[b], 16 * (2 * i + ((c - 8) // 4 - 2) // 2 + 1))
                        v.scalar_tensor_tensor(x4[b], psw[0], t2[:, bass.ds(96 + n, 1)], x3[b], ALU.add, ALU.add).then_inc(s_x4, 1)

            run_b(dve, b_slot)

        @block.scalar
        def _(act):
            a = nc.scalar
            act.wait_ge(s_red, 1)
            a.activation(sin[:, :, :], ang, ACT.Sin).then_inc(s_trig, 1)
            a.activation(cos[:, :, :], turn, ACT.Sin).then_inc(s_trig, 1)
            act.wait_ge(s_pre, 1)

            def a_slot(i, c):
                k = A_UN * i + c
                if valid(k, NT):
                    act.wait_ge(s_x1, k + 1)
                    a.copy(xall[:, k, :], x1s[c % 2]).then_inc(s_xc, 1)
                k = A_UN * i + c - 1
                b = (c - 1) % 2
                if valid(k, NT):
                    act.wait_ge(s_xt, k + 1)
                    wait(act, s_qkv, k - 1)
                    a.copy(x1t[b], psx[b][:, 0:D].rearrange("p (c t) -> p c t", c=2)).then_inc(s_xtc, 1)
                k = A_UN * i + c - 3
                b = (c - 3) % 2
                if valid(k, NT):
                    act.wait_ge(s_ss, k + 1)
                    wait(act, s_rc, k - 1)
                    a.activation(st[b][:, HEADS:2 * HEADS], st[b][:, 0:HEADS], ACT.Sqrt, bias=eps_c, scale=1.0 / HD).then_inc(s_st, 1)
                k = A_UN * i + c - 2
                b, r = (c - 2) % 2, (c - 2) % 4
                if valid(k, NT):
                    act.wait_ge(s_qkv, k + 1)
                    wait(act, s_ss, k - 1)
                    a.activation(sq[b], psq[b][:, 0:QK], ACT.Square).then_inc(s_sq, 1)
                    wait(act, s_scat[r], 16 * (i + (c - 6) // 4 + 1))
                    a.copy(qkvr[r][:, QK:QKV], psq[b][:, QK:QKV]).then_inc(s_v, 1)
                k = A_UN * i + c - 5
                b = (c - 5) % 2
                if valid(k, NT):
                    act.wait_ge(s_qt, k + 1)
                    a.copy(qt[:, k].rearrange("p b h t -> p h b t"),
                           psqt[b][:, 0:GSZ * P].rearrange("p (h b t) -> p h b t", h=GSZ, b=TB)).then_inc(s_qtc, 1)

            for n in range(3 * A_UN):
                a_slot(n // A_UN, n % A_UN)
            with act.Fori(3, NT // A_UN - 1) as i:
                for c in range(A_UN):
                    a_slot(i, c)
            for n in range(NT - A_UN, NT + 6):
                a_slot(n // A_UN, n % A_UN)

            act.wait_ge(s_pz, 2)

            def b_slot(i, c):
                w = c % GB
                g, par = 2 * i + c // GB + 1, (c // GB + 1) % 2
                if valid(g, NG) and w < 4:
                    act.wait_ge(s_kvt, GB * g + w + 1)
                    wait(act, s_kd[(par + 1) % 2], 256 * (i + 1))
                    a.copy(ka[:, w].rearrange("p (m o j) -> p m o j", m=2 * GB, o=4),
                           pskv[w % 2][:, 0:4 * WPX].rearrange("p (o m) -> p o m", o=4)[:, :, 0:WP]
                           .rearrange("p o (m j) -> p m o j", j=JH)).then_inc(s_kc, 1)
                U = 16 * i + c
                b = c % 2
                if valid(U, NU) and b == 1:
                    act.wait_ge(s_pt, U + 1)
                    wait(act, s_pv, U - 1)
                    a.copy(pts[b].rearrange("p g k -> p (g k)"), pspt[b][:, :]).then_inc(s_pc[1], 1)
                U = 16 * i + c + 1
                b = (c + 1) % 2
                if valid(U, NU):
                    n, g = 4 * i + (c + 1) // 4, (c + 1) % G
                    act.wait_ge(s_nm, U + 1)
                    wait(act, s_pt, U - 1)
                    wait(act, s_rl, n - 1)
                    for q in range(2):
                        e = a.activation(prob[b][:, q].rearrange("p h (o j) -> p (h o) j", j=8)[:, :, 0:JH],
                                         smx[b][:, q].rearrange("p (o j) -> p o j", j=JH), ACT.Exp,
                                         bias=nmax[b][:, q:q + 1],
                                         accum_out=rsum[((c + 1) // 4) % 2][:, G * q + g:G * q + g + 1])
                    e.then_inc(s_e, 1)
                if c % 4 == 1:
                    n, b = 4 * i + (c - 5) // 4, ((c - 5) // 4) % 2
                    if valid(n, NT):
                        act.wait_ge(s_ot, n + 1)
                        wait(act, s_wo, n - 1)
                        a.copy(ot[b], psot.rearrange("p (b h t) -> p h b t", b=TB, h=GSZ)).then_inc(s_oc, 1)

            run_b(act, b_slot)

        @block.tensor
        def _(pe):
            mm = nc.tensor.matmul
            pe.wait_ge(s_pairs, 1)
            for m, bank in ((later, ps[0]), (same, ps[1])):
                for s in range(NI):
                    for r in range(NI):
                        last = mm(bank[:, 16 * s:16 * s + 16], m[:, r].rearrange("p (b s) -> p s b", s=NI)[:, s],
                                  cov[:, 16 * r:16 * r + 16], start=(r == 0), stop=(r == NI - 1))
            last.then_inc(s_cnt, 1)
            pe.wait_ge(s_m, 80)
            nc.tensor.transpose(ps[2][:, 0:P], m1, ident)
            nc.tensor.transpose(ps[3][:, 0:P], m2, ident).then_inc(s_mt, 1)
            pe.wait_ge(s_wts, 32)
            pe.wait_ge(s_x, 16)
            pe.wait_ge(s_tidx, 1)

            def a_slot(i, c):
                k = A_UN * i + c
                b = c % 2
                if valid(k, NT):
                    pe.wait_ge(s_wbd, k + 1)
                    wait(pe, s_x1, k - 1)
                    mm(psl[b][:, 0:D], wbd[b], xall[:, k, :], start=True, stop=True).then_inc(s_l0, 1)
                k = A_UN * i + c - 1
                b = (c - 1) % 2
                if valid(k, NT):
                    pe.wait_ge(s_x1, k + 1)
                    wait(pe, s_xtc, k - 1)
                    nc.tensor.transpose(psx[b][:, 0:P], x1s[b][:, 0:P], ident)
                    nc.tensor.transpose(psx[b][:, P:2 * P], x1s[b][:, P:2 * P], ident).then_inc(s_xt, 1)
                k = A_UN * i + c - 2
                b = (c - 2) % 2
                if valid(k, NT):
                    pe.wait_ge(s_xtc, k + 1)
                    wait(pe, s_qn, k - 1)
                    wait(pe, s_v, k - 1)
                    for d in range(2):
                        last = mm(psq[b][:, :], x1t[b][:, d], wqkv_sb[:, d, :], start=(d == 0), stop=(d == 1))
                    last.then_inc(s_qkv, 1)
                k = A_UN * i + c - 5
                b, r = (c - 5) % 2, (c - 5) % 4
                if valid(k, NT):
                    pe.wait_ge(s_qr, 2 * k + 2)
                    wait(pe, s_qtc, k - 1)
                    q = qkvr[r][:, 0:H * HD].rearrange("p (h e) -> p h e", h=GSZ)
                    for h in range(GSZ):
                        last = nc.tensor.transpose(psqt[b][:, P * h:P * (h + 1)], q[:, h], ident)
                    last.then_inc(s_qt, 1)

            for n in range(3 * A_UN):
                a_slot(n // A_UN, n % A_UN)
            with pe.Fori(3, NT // A_UN - 1) as i:
                for c in range(A_UN):
                    a_slot(i, c)
            for n in range(NT - A_UN, NT + 6):
                a_slot(n // A_UN, n % A_UN)

            pe.wait_ge(s_qtc, NT)

            def keys_of(r, q, bb):
                return ktr[r:r + HD, q, 2 * bb:2 * bb + 2]

            def b_slot(i, c):
                U = 16 * i + c + 1
                b, q = (c + 1) % 2, ((c + 1) // GB) % 2
                if valid(U, NU):
                    g8 = 2 * i + (c + 1) // GB
                    pe.wait_ge(s_qs, g8 + 1)
                    pe.wait_ge(s_kd[q], 256 * (i + (c + 1) // 16 + 1))
                    wait(pe, s_sm, U - 1)
                    r = HD * ((c + 1) % G)
                    for k in range(2):
                        for e in range(2):
                            bb = TB * (((c + 1) % GB) // 4) + 2 * k + e
                            last = mm(pss[b][64 * e:64 * e + 64, KEYS * k:KEYS * (k + 1)],
                                      qs[q][r:r + HD, 64 * bb:64 * bb + 64],
                                      keys_of(r, q, bb), start=True, stop=True)
                    last.then_inc(s_s, 1)
                w = c % GB
                g8, par = 2 * i + c // GB + 1, (c // GB + 1) % 2
                if valid(g8, NG):
                    if w == 0:
                        pe.wait_ge(s_win[par], 32 * (i + (c // GB + 1) // 2 + 1))
                    if w < 2:
                        wait(pe, s_vc, 4 * g8 - 4 + w + 3)
                    elif w < 6:
                        pe.wait_ge(s_kc, 4 * g8 + w - 1)
                    else:
                        pe.wait_ge(s_vc, 4 * g8 + w - 5)
                    for o in range(4):
                        first = BLOCK * HD * (w % 4) + P * o
                        src = arena[0:WPX, par, w // 4, first:first + P]
                        last = nc.tensor.transpose(pskv[w % 2][:, WPX * o:WPX * (o + 1)], src, ident[0:WPX, 0:WPX])
                    last.then_inc(s_kvt, 1)
                U = 16 * i + c
                b = c % 2
                if valid(U, NU):
                    pe.wait_ge(s_e, U + 1)
                    wait(pe, s_pc[b], GB * i + c // 2)
                    for k in range(4):
                        last = nc.tensor.transpose(pspt[b][:, P * k:P * (k + 1)], prob[b][:, k // 2, k % 2], ident)
                    last.then_inc(s_pt, 1)
                U = 16 * i + c - 1
                b, q = (c - 1) % 2, ((c - 1) // GB) % 2
                if valid(U, NU):
                    n, g = 4 * i + (c - 1) // 4, (c - 1) % G
                    pe.wait_ge(s_pc[b], GB * i + (c - 1) // 2 + 1)
                    pe.wait_ge(s_vc, 4 * (2 * i + (c - 1) // GB) + 4)
                    if g == 0:
                        wait(pe, s_on, n)
                    for k in range(2):
                        col = P * k + HD * g
                        for e in range(2):
                            bb = TB * (((c - 1) % GB) // 4) + 2 * k + e
                            for h in range(2):
                                last = mm(pso[64 * e:64 * e + 64, col:col + HD], pts[b][:, 2 * k + h, 64 * e:64 * e + 64],
                                          vkeys[:, q, 2 * bb + h, HD * g:HD * (g + 1)], start=(h == 0), stop=(h == 1))
                    last.then_inc(s_pv, 1)
                if c % 4 == 1:
                    n, b = 4 * i + (c - 5) // 4, ((c - 5) // 4) % 2
                    if valid(n, NT):
                        pe.wait_ge(s_on, n + 1)
                        wait(pe, s_x4, n)
                        for k in range(2):
                            last = nc.tensor.transpose(psot[:, P * k:P * (k + 1)], on[b][:, P * k:P * (k + 1)], ident)
                        last.then_inc(s_ot, 1)
                if c % 4 == 2:
                    n, b = 4 * i + (c - 6) // 4, ((c - 6) // 4) % 2
                    if valid(n, NT):
                        pe.wait_ge(s_oc, n + 1)
                        for h in range(GSZ):
                            last = mm(psw[0], ot[b][:, h].rearrange("p b t -> p (b t)"), wo_sb[:, h, :], start=(h == 0), stop=(h == 1))
                        last.then_inc(s_wo, 1)
                if c % 4 == 3:
                    n, b = 4 * i + (c - 7) // 4, ((c - 7) // 4) % 2
                    if valid(n, NT):
                        pe.wait_ge(s_x2, n + 1)
                        pe.wait_ge(s_w23, 2 * n + 2)
                        wait(pe, s_x3, n)
                        mm(psw[1], wbd2[b], x2[b], start=True, stop=True).then_inc(s_l2, 1)
                if c % 4 == 0:
                    n, b = 4 * i + (c - 8) // 4, ((c - 8) // 4) % 2
                    if valid(n, NT):
                        pe.wait_ge(s_x3, n + 1)
                        mm(psw[0], wbd3[b], x3[b], start=True, stop=True).then_inc(s_l3, 1)

            run_b(pe, b_slot)


def kernel(**inputs):
    import concourse.bacc as _bacc
    from concourse import mybir as _mybir
    from concourse.bass_utils import run_bass_kernel_spmd as _run

    a = {k: np.ascontiguousarray(v) for k, v in inputs.items()}
    wqkv = np.concatenate([a["L1_cond_Wq"].reshape(G, GSZ, HD, D).transpose(1, 0, 2, 3).reshape(H * HD, D), a["L1_cond_Wk"], a["L1_cond_Wv"]], 0).T
    wqkv = wqkv.reshape(2, P, QKV).transpose(1, 0, 2)
    wo = a["L1_cond_Wo"].T.reshape(G, GSZ, HD, D).transpose(0, 2, 1, 3).reshape(P, GSZ, D)
    arrays = {
        "x": a["x"], "conditions": a["itok_B_1_198"], "tables": a["itok_Bx257_0_4111"], "kv_lens": a["itok_B_37_3939"],
        "subjects": a["itok_B_0_7"], "bias": a["fside_8xS_0"], "w0": a["L0_cond_weights"], "w2": a["L2_cond_weights"],
        "w3": a["L3_cond_weights"], "wqkv": wqkv, "wo": wo, "q_scale": a["L1_cond_q_norm_scale"],
        "k_scale": a["L1_cond_k_norm_scale"], "k_cache": a["L1_cond_k_blocks"], "v_cache": a["L1_cond_v_blocks"],
        "consts": constants(),
    }
    arrays = {k: np.ascontiguousarray(v) for k, v in arrays.items()}
    nc = _bacc.Bacc("TRN2", target_bir_lowering=False, num_devices=1)
    args = [nc.dram_tensor(k, v.shape, _mybir.dt.from_np(v.dtype), kind="ExternalInput").ap() for k, v in arrays.items()]
    out = nc.dram_tensor("out", (B, T, D), F32, kind="ExternalOutput").ap()
    build(nc, *args, out)
    r = _run(nc, [arrays], core_ids=[0])
    return r.results[0]["out"]
```

```python
import math
from contextlib import ExitStack

import numpy as np
import concourse.bass as bass
from concourse import mybir

F32 = mybir.dt.float32
I32 = mybir.dt.int32
ALU = mybir.AluOpType
ACT = mybir.ActivationFunctionType
AX = mybir.AxisListType

P = 128
B, T, D = 128, 32, 256
H, G, HD = 8, 4, 32
GSZ = H // G
BLOCK, WINDOW = 16, 128
SUBJ = 8
EPS = 1e-6
TB = P // T
NT = B // TB
SPAN = WINDOW // BLOCK
NI = 3
SLOTS = SPAN + NI
JH = (SLOTS + 1) // 2
WS = 2 * JH
GB = 8
NG = B // GB
WP = GB * WS
WPX = (2 * GB - 1) * JH + 8
KEYS = WS * BLOCK
BE = G * BLOCK * HD
FAR = 1.0e6
MASKED = 2.0 ** 100
HEADS = H + G
QK = HEADS * HD
QKV = QK + G * HD

C_ID, C_BM, C_KAP, C_INV, C_IOTA, C_ITEM = 0, 128, 132, 132 + KEYS, 148 + KEYS, 148 + KEYS + 388
C_END = C_ITEM + NI


def constants():
    c = np.zeros((P, C_END), np.float32)
    p = np.arange(P)
    c[:, C_ID:C_ID + P] = np.eye(P)
    c[:, C_BM:C_BM + TB] = (p[:, None] // T == np.arange(TB))
    h, r, o, j = np.meshgrid(np.arange(2), np.arange(4), np.arange(4), np.arange(JH), indexing="ij")
    c[:, C_KAP:C_KAP + KEYS] = MASKED * ((JH * h + j) * BLOCK + 4 * o + r).reshape(-1)
    half = HD // 2
    c[:, C_INV:C_INV + half] = np.float32(1.0) / np.float32(10000.0) ** (np.arange(half, dtype=np.float32) / np.float32(half))
    c[:, C_IOTA:C_IOTA + 388] = np.arange(388)
    c[:, C_ITEM:C_ITEM + NI] = NI * p[:, None] + np.arange(NI)
    return c


def valid(index, count):
    return not isinstance(index, int) or 0 <= index < count


def wait(eng, sem, value):
    if not isinstance(value, int) or value > 0:
        eng.wait_ge(sem, value)


def wait_first(eng, sem, value, passed):
    wait(eng, sem, value)
    if not isinstance(value, int):
        eng.sem_inc(passed, 1)


def build(nc, x, conditions, tables, kv_lens, subjects, bias, w0, w2, w2t, w3, wqkv, wo, q_scale, k_scale,
          k_cache, v_cache, consts, out):
    NBLK = tables.shape[1]
    NCACHE = k_cache.shape[0]
    ctx = ExitStack()
    with ctx:
        def sb(name, shape, dt=F32):
            return ctx.enter_context(nc.sbuf_tensor(name, shape, dt))

        def sem(name):
            return ctx.enter_context(nc.semaphore(name))

        d_w = [nc.dram_tensor(f"d_w{k}", (B, T * T), F32).ap() for k in range(2)]
        d_w23 = nc.dram_tensor("d_w23", (SUBJ, T * T), F32).ap()
        d_item = nc.dram_tensor("d_item", (B, NI), F32).ap()
        d_m1 = nc.dram_tensor("d_m1", (P, P), F32).ap()
        d_m2 = nc.dram_tensor("d_m2", (P, P), F32).ap()
        d_win = nc.dram_tensor("d_win", (2, B, WS), F32).ap()
        new_rows = nc.dram_tensor("new_rows", (B * NI * BLOCK, 2 * G * HD), F32).ap()
        patched = [nc.dram_tensor(f"patched_{k}", (B * NI, BE), F32).ap() for k in "kv"]

        xall = sb("xall", [P, NT, D])
        qt = sb("qt", [P, NT, TB, GSZ, T])
        wc = [sb(f"wc{k}", [P, NT, T]) for k in range(2)]
        xmix = [sb(f"xmix{k}", [P, T * T]) for k in range(2)]
        wsubj = sb("wsubj", [T, 4, SUBJ, T])
        wqkv_sb = sb("wqkv_sb", [P, 2, QKV])
        wo_sb = sb("wo_sb", [P, GSZ, D])
        cst = sb("cst", [P, C_END])
        gain = sb("gain", [P, HEADS, HD])
        scales = sb("scales", [P, 2, HD])
        cos = sb("cos", [P, NT, HD // 2])
        sin = sb("sin", [P, NT, HD // 2])
        t1 = sb("t1", [P, P])
        t2 = sb("t2", [P, P])
        toki = sb("toki", [P, NT], I32)
        wini = sb("wini", [P, 2, NG], I32)
        bounds = sb("bounds", [P, B // 2, 3])
        rowi = sb("rowi", [P, 4], I32)
        blki = sb("blki", [P, 2, 2], I32)
        arena = sb("arena", [P, 4, 2, BE])
        stage = arena[:, 3].rearrange("p a (h o e) -> p (a h) o e", h=1, o=BLOCK // 2)
        vkeys = arena[:, 2].rearrange("p a (m e) -> p a m e", m=2 * GB)
        ktr = arena[:, 3, :, 0:WP * BLOCK]
        ktr = ktr.rearrange("p a (r m e) -> p a m r e", r=4, m=2 * GB)

        ident = cst[:, C_ID:C_ID + P]
        bmask = cst[:, C_BM:C_BM + TB]
        kappa = cst[:, C_KAP:C_KAP + KEYS]
        inv = cst[:, C_INV:C_INV + HD // 2]

        def iota(n, first=0):
            return cst[:, C_IOTA + first:C_IOTA + first + n]

        WORK = 10240
        work = sb("work", [P, WORK])
        small = sb("small", [P, 512])
        smalli = sb("smalli", [P, 16], I32)
        at = [0]

        def cut(n, dt=None):
            a = work[:, at[0]:at[0] + n]
            at[0] += n
            assert at[0] <= WORK, at[0]
            return a

        tab_f = cut(NBLK + 3)[:, 0:NBLK]
        tab_i = cut(NBLK + 3)[:, 0:NBLK].bitcast(I32)
        pick = cut(NBLK + 3)[:, 0:NBLK]
        item_row = cut(B * NI)
        same = cut(NI * B * NI).rearrange("p (s i) -> p s i", s=NI)
        later = cut(NI * B * NI).rearrange("p (s i) -> p s i", s=NI)
        repm = cut(B * NI)
        m1 = cut(P)
        m2 = cut(P)
        pack = cut(32 + 32 + 64 + 64 + 2 * WS)
        p_tok, p_pos = pack[:, 0:32], pack[:, 32:64]
        p_up = pack[:, 64:128].rearrange("p (h t) -> p h t", h=GSZ)
        p_low = pack[:, 128:192].rearrange("p (h t) -> p h t", h=GSZ)
        p_win = pack[:, 192:192 + 2 * WS].rearrange("p (k j) -> p k j", k=2)
        ang = cut(NT * (HD // 2)).rearrange("p (n d) -> p n d", n=NT)
        turn = cut(NT * (HD // 2)).rearrange("p (n d) -> p n d", n=NT)
        biasg = cut(T)
        at[0] = 0
        wbd = [cut(P) for _ in range(2)]
        x1s = [cut(D) for _ in range(2)]
        x1t = [cut(D).rearrange("p (c t) -> p c t", c=2) for _ in range(2)]
        sq = [cut(QK) for _ in range(2)]
        qn = [cut(QK) for _ in range(2)]
        qg = [cut(QK) for _ in range(2)]
        ra = [cut(QK) for _ in range(2)]
        rb = [cut(QK) for _ in range(2)]
        qkvr = [cut(QKV) for _ in range(4)]
        st = [cut(3 * HEADS) for _ in range(2)]
        at[0] = 0
        qs = [cut(GB * GSZ * T) for _ in range(2)]
        msk = [cut(2 * KEYS) for _ in range(2)]
        mska = cut(2 * KEYS).rearrange("p (q k) -> p q k", q=2)
        smx = [cut(2 * KEYS).rearrange("p (q k) -> p q k", q=2) for _ in range(2)]
        prob = [cut(4 * P).rearrange("p (q h k) -> p q h k", q=2, h=2) for _ in range(2)]
        pts = [cut(4 * P).rearrange("p (g k) -> p g k", g=4) for _ in range(2)]
        on = [cut(2 * P) for _ in range(2)]
        ot = [cut(GSZ * P).rearrange("p (h b t) -> p h b t", h=GSZ, b=TB) for _ in range(2)]
        wbd2 = [cut(P) for _ in range(2)]
        x2 = [cut(D) for _ in range(2)]
        x4 = [cut(D) for _ in range(2)]
        ka = cut(G * 4 * WP).rearrange("p (g k) -> p g k", g=G)
        nmax = [cut(2) for _ in range(2)]
        rsum = [cut(2 * G) for _ in range(2)]
        rinv = [cut(2 * G) for _ in range(2)]

        kv_i, f_i, s_i, sub_i, con_i = (smalli[:, k:k + 1] for k in range(5))
        blk_i = smalli[:, 8:8 + NI]
        kv_f, f_f, s_f, f32_f, low_f = (small[:, k:k + 1] for k in range(5))
        eps_c = small[:, 5:6]
        sidx = small[:, 8:8 + SLOTS]
        blk = small[:, 24:24 + SLOTS]
        rep = small[:, 40:40 + SLOTS]
        hit = small[:, 56:56 + SLOTS]
        base = small[:, 72:72 + NI]
        fmask = small[:, 80:96]
        cov = small[:, 96:144]
        wins = small[:, 144:192]
        keep = small[:, 192:240]
        cell = small[:, 240:288]
        ft = small[:, 288:320]
        tmp48 = small[:, 320:368]
        miss = small[:, 368:368 + SLOTS]

        ps = [ctx.enter_context(nc.psum_tensor(f"ps{k}", [P, 512], F32)) for k in range(8)]

        s_kv, s_tab, s_cs, s_idx, s_cst = sem("kv_loaded"), sem("tables_loaded"), sem("choices_loaded"), sem("items_stored"), sem("consts_loaded")
        s_x, s_wts, s_scl = sem("x_loaded"), sem("weights_loaded"), sem("scales_loaded")
        s_mixg, s_mixd, s_mix = sem("mixes_gathered"), sem("mixes_stored"), sem("mixes_loaded")
        s_itemrow, s_blk, s_blki = sem("item_row_loaded"), sem("blocks_found"), sem("block_indices")
        s_itemg = sem("item_blocks_gathered")
        s_zero, s_zeroed = sem("zero_tile"), sem("new_rows_zeroed")
        s_pairs, s_cnt = sem("item_pairs"), sem("later_counts")
        s_pack, s_packd, s_m = sem("pack_ready"), sem("pack_stored"), sem("matrices_loaded")
        s_mz, s_mt, s_tidx = sem("matrix_cleared"), sem("matrices_transposed"), sem("indices_ready")
        s_trig, s_red = sem("angles_done"), sem("angles_reduced")
        s_dve = sem("vector_step")
        s_wsubj, s_w23p, s_w23s, s_w23d = sem("mixes_loaded_by_subject"), sem("mix_products"), sem("mixes_combined"), sem("combined_mixes_stored")
        s_gain, s_masked = sem("gain_ready"), sem("old_rows_masked")
        s_pre = sem("prelude_done")
        s_wbd, s_l0, s_x1, s_xc, s_xt, s_xtc, s_qkv = (sem(n) for n in ("mix0_ready", "mix0_done", "x1_ready", "x1_kept", "x1_transposed", "x1t_ready", "qkv_done"))
        s_sq, s_v, s_ss, s_st, s_rc, s_qn, s_qg, s_ra, s_rb, s_qr, s_qt, s_qtc = (sem(n) for n in (
            "squares", "v_copied", "square_sums", "norms", "norm_recips", "normed", "gained", "rope_cos", "rope_sin",
            "qk_ready", "q_transposed", "qt_ready"))
        s_scat = [sem(f"rows_scattered{k}") for k in range(4)]
        s_stage = [sem(f"new_rows_loaded{k}") for k in range(2)]
        s_addk, s_addv, s_patched = sem("k_patched"), sem("v_patched"), sem("patched_stored")
        s_old = [sem(f"old_blocks_loaded{k}") for k in range(2)]
        s_win = [sem(f"window_loaded{k}") for k in range(2)]
        s_kvt, s_kc, s_vc, s_qs = sem("window_transposed"), sem("keys_ready"), sem("values_ready"), sem("queries_staged")
        s_kd = [sem(f"keys_moved{k}") for k in range(2)]
        s_passed = [sem("gpsimd_passed"), sem("sync_passed"), sem("vector_passed")]
        s_ma, s_mk = sem("mask_parts"), sem("mask_ready")
        s_s, s_sm, s_e, s_pt, s_pv = (sem(n) for n in (
            "scores", "masked_scores", "probs", "probs_transposed", "pv_done"))
        s_rl, s_on, s_ot, s_oc, s_wo, s_w23 = (sem(n) for n in ("sum_recips", "o_normed", "o_transposed", "ot_ready", "wo_done", "mix23_ready"))
        s_x2, s_l2, s_x4 = (sem(n) for n in ("x2_ready", "mix23_done", "x4_ready"))
        s_out = [sem(f"out_stored{k}") for k in range(2)]
        s_pc = [sem(f"probs_t_ready{k}") for k in range(2)]
        s_pz, s_ri, s_bi = sem("probs_cleared"), sem("row_indices"), sem("window_indices")

        psl, psx, psq, psqt = ps[0:2], ps[2:4], ps[4:6], ps[6:8]
        pss, pspt, pskv = ps[0:4], ps[4], ps[5]
        pso, psot = ps[6], ps[7][:, 0:256]
        psw = [ps[7][:, 256:512], ps[7][:, 0:256]]

        xv = x.rearrange("(n b) c t -> (b c) n t", b=TB)
        outv = out.rearrange("(n b) c t -> n (b c) t", b=TB)
        mixv = [d.rearrange("(n b) (c d) -> (b c) n d", b=TB, c=T) for d in d_w]
        rowsv = new_rows.rearrange("(b s o) e -> s b o e", s=NI, o=BLOCK)
        patchedv = [d.rearrange("(b s) e -> s b e", s=NI) for d in patched]
        cachev = [c.rearrange("n g o d -> n (g o d)") for c in (k_cache, v_cache)]

        A_UN = 4
        NU = NG * GB

        block = ctx.enter_context(nc.Block())

        def store_item(sp, s):
            sp.wait_ge(s_addk, 2 * s + 2)
            sp.wait_ge(s_addv, 2 * s + 2)
            for k in range(2):
                sp.dma_start(patchedv[k][s], arena[:, s, k]).then_inc(s_patched, 16)

        def run_b(eng, slot):
            for i in (-1, 0):
                for c in range(16):
                    slot(i, c)
            with eng.Fori(1, NG // 2 - 1) as i:
                for c in range(16):
                    slot(i, c)
            for i in (NG // 2 - 1, NG // 2):
                for c in range(16):
                    slot(i, c)

        def ktr_rows(par, g, r):
            return arena[HD * g:HD * (g + 1), 3, par, 4 * WP * r:4 * WP * (r + 1)]

        def window_columns(bank):
            a = bank[:, 0:4 * WPX].rearrange("p (o m) -> p o m", o=4)
            lap = a[:, :, 0:8].unsqueeze(1).broadcast_to([P, 2 * GB, 4, 8])
            return bass.AP(tensor=lap.tensor, offset=lap.offset, ap=[lap.ap[0], [JH, 2 * GB], lap.ap[2], lap.ap[3]])

        @block.sync
        def _(sp):
            sp.dma_start(kv_i, kv_lens.unsqueeze(1)).then_inc(s_kv, 16)
            sp.dma_start(sub_i, subjects.unsqueeze(1)).then_inc(s_cs, 16)
            sp.dma_start(con_i, conditions.unsqueeze(1)).then_inc(s_cs, 16)
            sp.dma_start(cst[:, :], consts).then_inc(s_cst, 16)
            for k, w in enumerate((w2, w2t, w3)):
                sp.dma_start(wsubj[:, k], w.rearrange("s c d -> c s d")).then_inc(s_wsubj, 16)
            sp.dma_start(tab_i, tables).then_inc(s_tab, 16)
            sp.dma_start(scales[:, 0], q_scale.partition_broadcast(P)).then_inc(s_scl, 16)
            sp.dma_start(scales[:, 1], k_scale.partition_broadcast(P)).then_inc(s_scl, 16)
            sp.dma_start(xall[:, :, :], xv).then_inc(s_x, 16)
            sp.dma_start(wqkv_sb[:, :, :], wqkv).then_inc(s_wts, 16)
            sp.dma_start(wo_sb[:, :, :], wo).then_inc(s_wts, 16)
            sp.wait_ge(s_blk, 1)
            sp.dma_start(d_item, blk[:, SPAN:SLOTS]).then_inc(s_idx, 16)
            sp.wait_ge(s_w23s, 2)
            sp.dma_start(d_w23.rearrange("s (c d) -> c s d", c=T), wsubj[:, 3]).then_inc(s_w23d, 16)
            sp.wait_ge(s_mixg, 48)
            for k in range(2):
                sp.dma_start(d_w[k], xmix[k][:, :]).then_inc(s_mixd, 16)
            sp.dma_start(d_m2[96:128, :].rearrange("n (b t) -> (n b) t", b=TB), biasg).then_inc(s_mixd, 16)
            sp.wait_ge(s_idx, 16)
            sp.dma_start(item_row, d_item.rearrange("b s -> (b s)").partition_broadcast(P)).then_inc(s_itemrow, 16)
            sp.wait_ge(s_mixd, 48)
            for k in range(2):
                sp.dma_start(wc[k][:, :, :], mixv[k]).then_inc(s_mix, 16)
            sp.wait_ge(s_zero, 1)
            for s in range(NI):
                sp.dma_start(rowsv[s], arena[:, 3].rearrange("p a e -> p (a e)")
                             .rearrange("p (o e) -> p o e", o=BLOCK)).then_inc(s_zeroed, 16)
            sp.wait_ge(s_pack, 1)
            sp.dma_start(d_m1[0:32, :].rearrange("n (b t) -> (n b) t", b=TB), p_tok).then_inc(s_packd, 16)
            sp.dma_start(d_m1[32:64, :].rearrange("n (b t) -> (n b) t", b=TB), p_pos).then_inc(s_packd, 16)
            sp.dma_start(d_m1[64:128, :].rearrange("n (b t) -> (n b) t", b=2), pack[:, 64:128]).then_inc(s_packd, 16)
            sp.dma_start(d_m2[0:64, :].rearrange("n (b t) -> (n b) t", b=2), pack[:, 128:192]).then_inc(s_packd, 16)
            for k in range(2):
                sp.dma_start(d_win[k], p_win[:, k]).then_inc(s_packd, 16)
            sp.wait_ge(s_packd, 96)
            sp.wait_ge(s_mz, 1)
            sp.dma_start(m1, d_m1).then_inc(s_m, 16)
            sp.dma_start(m2[0:64, :], d_m2[0:64, :]).then_inc(s_m, 16)
            sp.dma_start(m2[96:128, :], d_m2[96:128, :]).then_inc(s_m, 16)
            for k in range(2):
                sp.dma_start(m2[64 + NG * k:64 + NG * (k + 1), 0:WP],
                             d_win[k].rearrange("(n b) j -> n (b j)", b=GB)).then_inc(s_m, 16)
            for k in range(4):
                sp.wait_ge(s_scat[k], 16 * (NT // 4))
            sp.wait_ge(s_zeroed, 48)
            for w in range(2 * NI):
                s, h = w // 2, w % 2
                if w >= 2:
                    sp.wait_ge(s_addk, w - 1)
                    sp.wait_ge(s_addv, w - 1)
                sp.dma_start(stage[:, w % 2], rowsv[s][:, 8 * h:8 * h + 8, :]).then_inc(s_stage[w % 2], 16)
                if w >= 3 and w % 2:
                    store_item(sp, (w - 3) // 2)
            store_item(sp, NI - 1)
            def b_slot(i, c):
                w = c % GB - 1
                g, par = 2 * i + c // GB + 1, (c // GB + 1) % 2
                if valid(g, NG) and 0 <= w < G:
                    wait_first(sp, s_kc, 4 * g + w + 1, s_passed[1])
                    wait(sp, s_s, G * (g - 1))
                    for r in range(4):
                        sp.dma_start(ktr_rows(par, w, r), ka[HD * r:HD * (r + 1), w]).then_inc(s_kd[par], 16)
                if c % 4 == 1:
                    n, b = 4 * i + (c - 9) // 4, ((c - 9) // 4) % 2
                    if valid(n, NT):
                        wait_first(sp, s_x4, n + 1, s_passed[1])
                        sp.dma_start(outv[n], x4[b]).then_inc(s_out[b], 16)
            run_b(sp, b_slot)
            for k in range(2):
                sp.wait_ge(s_out[k], 16 * (NT // 2))

        @block.gpsimd
        def _(pool):
            pool.memset(arena[:, 3], 0.0).then_inc(s_zero, 1)
            pool.memset(m2, 0.0).then_inc(s_mz, 1)
            pool.wait_ge(s_cs, 32)
            pool.indirect_dma_start(out=xmix[0][:, :], out_offset=None, in_=w0.rearrange("n c d -> n (c d)"),
                                    in_offset=bass.IndirectOffsetOnAxis(ap=con_i, axis=0),
                                    bounds_check=w0.shape[0] - 1, oob_is_err=False).then_inc(s_mixg, 16)
            pool.indirect_dma_start(out=biasg, out_offset=None, in_=bias,
                                    in_offset=bass.IndirectOffsetOnAxis(ap=sub_i, axis=0),
                                    bounds_check=SUBJ - 1, oob_is_err=False).then_inc(s_mixg, 16)
            pool.wait_ge(s_w23d, 16)
            pool.indirect_dma_start(out=xmix[1][:, :], out_offset=None, in_=d_w23,
                                    in_offset=bass.IndirectOffsetOnAxis(ap=sub_i, axis=0),
                                    bounds_check=SUBJ - 1, oob_is_err=False).then_inc(s_mixg, 16)
            pool.wait_ge(s_blki, 1)
            for s in range(NI):
                for k in range(2):
                    pool.indirect_dma_start(out=arena[:, s, k], out_offset=None, in_=cachev[k],
                                            in_offset=bass.IndirectOffsetOnAxis(ap=blk_i[:, s:s + 1], axis=0),
                                            bounds_check=NCACHE - 1, oob_is_err=False).then_inc(s_itemg, 16)
            pool.wait_ge(s_mix, 32)
            pool.wait_ge(s_gain, 1)

            def expand(dst, src, sm):
                nc.gpsimd.tensor_tensor(dst.rearrange("p (b d) -> p b d", b=TB),
                                        src.unsqueeze(1).broadcast_to([P, TB, T]),
                                        bmask.unsqueeze(2).broadcast_to([P, TB, T]), ALU.mult).then_inc(sm, 1)

            def a_slot(i, c):
                k = A_UN * i + c - 4
                if valid(k, NT):
                    b = (c - 4) % 2
                    pool.wait_ge(s_qn, k + 1)
                    wait(pool, s_rb, 2 * k - 2)
                    wait(pool, s_ra, k - 1)
                    nc.gpsimd.tensor_tensor(qg[b], qn[b], gain[:, :, :].rearrange("p h d -> p (h d)"), ALU.mult).then_inc(s_qg, 1)
                    pool.wait_ge(s_qg, k + 1)
                    wait(pool, s_qr, 2 * k - 2)
                    nc.gpsimd.tensor_tensor(ra[b].rearrange("p (h d) -> p h d", d=HD // 2),
                                            qg[b].rearrange("p (h d) -> p h d", d=HD // 2),
                                            cos[:, k, :].unsqueeze(1).broadcast_to([P, 2 * HEADS, HD // 2]),
                                            ALU.mult).then_inc(s_ra, 1)
                k = A_UN * i + c + 1
                if valid(k, NT):
                    wait(pool, s_l0, k - 1)
                    expand(wbd[(c + 1) % 2], wc[0][:, k, :], s_wbd)
                k = A_UN * i + c - 5
                if valid(k, NT):
                    r = (c - 5) % 4
                    pool.wait_ge(s_qr, 2 * k + 2)
                    pool.wait_ge(s_v, k + 1)
                    wait(pool, s_scat[r], 16 * (i + (c - 9) // 4 + 1))
                    nc.gpsimd.tensor_copy(rowi[:, r:r + 1], toki[:, bass.ds(k, 1)]).then_inc(s_ri, 1)
                    wait_first(pool, s_ri, k + 1, s_passed[0])
                    pool.indirect_dma_start(out=new_rows,
                                            out_offset=bass.IndirectOffsetOnAxis(ap=rowi[:, r:r + 1], axis=0),
                                            in_=qkvr[r][:, H * HD:QKV], in_offset=None,
                                            bounds_check=B * NI * BLOCK - 1, oob_is_err=False).then_inc(s_scat[r], 16)

            pool.wait_ge(s_pre, 1)
            expand(wbd[0], wc[0][:, 0, :], s_wbd)
            pool.wait_ge(s_zeroed, 48)
            pool.wait_ge(s_trig, 2)
            for n in range(3 * A_UN):
                a_slot(n // A_UN, n % A_UN)
            with pool.Fori(3, NT // A_UN - 1) as i:
                for c in range(A_UN):
                    a_slot(i, c)
            for n in range(NT - A_UN, NT + 6):
                a_slot(n // A_UN, n % A_UN)

            for w in range(2 * NI):
                s, h = w // 2, w % 2
                pool.wait_ge(s_stage[w % 2], 16 * (w // 2 + 1))
                pool.wait_ge(s_masked, 2 * NI)
                o = arena[:, s, 1].rearrange("p (g o d) -> p g o d", g=G, o=BLOCK)[:, :, 8 * h:8 * h + 8, :]
                nc.gpsimd.tensor_tensor(o, o, stage[:, w % 2, :, G * HD:2 * G * HD]
                                        .rearrange("p o (g d) -> p g o d", g=G), ALU.add).then_inc(s_addv, 1)

            def b_slot(i, c):
                if c % GB == 0:
                    g, par = 2 * i + c // GB + 2, (c // GB) % 2
                    if valid(g, NG):
                        if isinstance(g, int) and g < 2:
                            pool.wait_ge(s_patched, 32 * NI)
                        wait(pool, s_kvt, GB * (g - 1))
                        wait(pool, s_win[par], 32 * (i + 1))
                        nc.gpsimd.tensor_copy(blki[0:WP, par], wini[0:WP, :, bass.ds(g, 1)].rearrange("p k a -> p (k a)")).then_inc(s_bi, 1)
                        wait_first(pool, s_bi, g + 1, s_passed[0])
                        for k in range(2):
                            pool.indirect_dma_start(out=arena[0:WP, par, k], out_offset=None, in_=cachev[k],
                                                    in_offset=bass.IndirectOffsetOnAxis(ap=blki[0:WP, par, 0:1], axis=0),
                                                    bounds_check=NCACHE - 1, oob_is_err=False).then_inc(s_old[par], 16)
                if c % GB == 2:
                    g, par = 2 * i + c // GB + 2, (c // GB) % 2
                    if valid(g, NG):
                        wait_first(pool, s_old[par], 32 * (i + 2), s_passed[0])
                        for k in range(2):
                            pool.indirect_dma_start(out=arena[0:WP, par, k], out_offset=None, in_=patched[k],
                                                    in_offset=bass.IndirectOffsetOnAxis(ap=blki[0:WP, par, 1:2], axis=0),
                                                    bounds_check=B * NI - 1, oob_is_err=False).then_inc(s_win[par], 16)
                if c % GB == 1:
                    g, par = 2 * i + c // GB + 1, (c // GB + 1) % 2
                    if valid(g, NG):
                        wait(pool, s_s, G * (g - 1))
                        if isinstance(g, int) and g == 0:
                            pool.wait_ge(s_qtc, NT)
                        nc.gpsimd.tensor_copy(qs[par], qt[:, bass.ds(2 * g, 2)].rearrange("p n b h t -> p (n b h t)")).then_inc(s_qs, 1)
                if c % 4 == 0:
                    n, par = 4 * i + c // 4 - 1, (c // 4 - 1) % 2
                    if valid(n, NT):
                        wait(pool, s_l2, n - 1)
                        expand(wbd2[par], wc[1][:, bass.ds(n, 1), :].rearrange("p a d -> p (a d)"), s_w23)

            pool.wait_ge(s_qtc, NT)
            for b in range(2):
                nc.gpsimd.memset(prob[b].rearrange("p g h k -> p (g h k)"), 0.0).then_inc(s_pz, 1)
            run_b(pool, b_slot)

        @block.vector
        def _(dve):
            v = nc.vector
            steps = [0]

            def link(ins):
                steps[0] += 1
                ins.then_inc(s_dve, 1)
                dve.wait_ge(s_dve, steps[0])

            dve.wait_ge(s_kv, 16)
            dve.wait_ge(s_cst, 16)
            v.tensor_scalar(f_i, kv_i, BLOCK - 1, None, ALU.bitwise_and)
            link(v.tensor_scalar(s_i, kv_i, int(math.log2(BLOCK)), None, ALU.arith_shift_right))
            v.tensor_copy(kv_f, kv_i)
            v.tensor_copy(f_f, f_i)
            link(v.tensor_copy(s_f, s_i))
            link(v.tensor_scalar(sidx, iota(SLOTS), s_f, float(-SPAN), ALU.add, ALU.add))
            link(v.tensor_scalar(sidx, sidx, 0.0, float(NBLK - 1), ALU.max, ALU.min))
            dve.wait_ge(s_tab, 16)
            link(v.tensor_copy(tab_f, tab_i))
            for j in range(SLOTS):
                link(v.scalar_tensor_tensor(pick, iota(NBLK), sidx[:, j:j + 1], tab_f, ALU.is_equal, ALU.mult,
                                            accum_out=blk[:, j:j + 1]))
            link(v.tensor_copy(blk_i, blk[:, SPAN:SLOTS]))
            v.sem_inc(s_blk, 1)
            v.sem_inc(s_blki, 1)
            dve.wait_ge(s_w23p, 1)
            link(v.tensor_tensor(wsubj[:, 3].rearrange("c s d -> c (s d)"), ps[6][0:T, 0:SUBJ * T],
                                 wsubj[:, 0].rearrange("c s d -> c (s d)"), ALU.add))
            v.sem_inc(s_w23s, 1)
            link(v.tensor_tensor(wsubj[:, 3], wsubj[:, 3], wsubj[:, 2], ALU.add))
            v.sem_inc(s_w23s, 1)
            link(v.tensor_scalar(f32_f, f_f, float(T), None, ALU.add))
            link(v.tensor_scalar(tmp48, iota(NI * BLOCK), f_f, None, ALU.is_ge))
            link(v.scalar_tensor_tensor(cov, iota(NI * BLOCK), f32_f, tmp48, ALU.is_lt, ALU.mult))
            dve.wait_ge(s_itemrow, 16)
            for s in range(NI):
                link(v.tensor_scalar(same[:, s], item_row, blk[:, SPAN + s:SPAN + s + 1], None, ALU.is_equal))
                link(v.scalar_tensor_tensor(later[:, s], iota(B * NI), cst[:, C_ITEM + s:C_ITEM + s + 1], same[:, s],
                                            ALU.is_lt, ALU.mult))
            v.sem_inc(s_pairs, 1)
            for j in range(SLOTS):
                link(v.scalar_tensor_tensor(repm, item_row, blk[:, j:j + 1], iota(B * NI, 1), ALU.is_equal, ALU.mult))
                link(v.tensor_reduce(rep[:, j:j + 1], repm, AX.X, ALU.max))
            v.tensor_scalar(p_pos, iota(T), kv_f, None, ALU.add)
            link(v.tensor_scalar(ft, iota(T), f_f, None, ALU.add))
            link(v.tensor_scalar(low_f, s_f, float(-BLOCK), float(WINDOW - 1), ALU.mult, ALU.add))
            for h in range(GSZ):
                v.tensor_scalar(p_up[:, h], ft, float(WINDOW), None, ALU.add)
                v.tensor_scalar(p_low[:, h], ft, low_f, None, ALU.max)
            link(v.memset(p_win[:, 0], FAR))
            link(v.memset(p_win[:, 1], FAR))
            link(v.tensor_scalar(hit, rep, 0.0, None, ALU.is_gt))
            link(v.tensor_scalar(miss, rep, 0.0, None, ALU.is_equal))
            link(v.scalar_tensor_tensor(p_win[:, 0, 0:SLOTS], hit, FAR, blk, ALU.mult, ALU.add))
            link(v.scalar_tensor_tensor(miss, miss, FAR, rep, ALU.mult, ALU.add))
            link(v.tensor_scalar(p_win[:, 1, 0:SLOTS], miss, -1.0, None, ALU.add))
            dve.wait_ge(s_cnt, 1)
            link(v.scalar_tensor_tensor(wins, ps[0][:, 0:48], 0.0, cov, ALU.is_equal, ALU.mult))
            link(v.tensor_scalar(keep, ps[1][:, 0:48], 0.0, None, ALU.is_equal))
            link(v.tensor_scalar(base, rep[:, SPAN:SLOTS], float(BLOCK), -float(BLOCK) - FAR, ALU.mult, ALU.add))
            for s in range(NI):
                v.scalar_tensor_tensor(cell[:, 16 * s:16 * s + 16], iota(BLOCK), base[:, s:s + 1],
                                       wins[:, 16 * s:16 * s + 16], ALU.add, ALU.mult)
            link(v.tensor_scalar(fmask, iota(BLOCK), f_f, None, ALU.is_equal))
            link(v.tensor_scalar(cell, cell, FAR, None, ALU.add))
            link(v.tensor_scalar(p_tok, cell[:, 0:T], fmask[:, 0:1], None, ALU.mult))
            for f in range(1, BLOCK):
                link(v.scalar_tensor_tensor(p_tok, cell[:, f:f + T], fmask[:, f:f + 1], p_tok, ALU.mult, ALU.add))
            v.sem_inc(s_pack, 1)
            dve.wait_ge(s_scl, 32)
            link(v.tensor_scalar(gain[:, 0:H, :], scales[:, 0].unsqueeze(1).broadcast_to([P, H, HD]),
                                 1.0, 256.0 ** -0.5, ALU.add, ALU.mult))
            link(v.tensor_scalar(gain[:, H:HEADS, :], scales[:, 1].unsqueeze(1).broadcast_to([P, G, HD]),
                                 1.0, None, ALU.add))
            v.sem_inc(s_gain, 1)
            dve.wait_ge(s_mt, 1)
            v.tensor_copy(t1[:, :], ps[2][:, 0:P])
            link(v.tensor_copy(t2[:, :], ps[3][:, 0:P]))
            v.tensor_copy(toki[:, :], t1[:, 0:NT])
            v.tensor_scalar(bounds[:, :, 0], t1[:, 64:128], MASKED, None, ALU.mult)
            link(v.tensor_scalar(bounds[:, :, 1], t2[:, 0:64], 1.0, MASKED, ALU.add, ALU.mult))
            v.tensor_tensor(bounds[:, :, 2], bounds[:, :, 0], bounds[:, :, 1], ALU.subtract)
            link(v.tensor_copy(wini[:, :, :].rearrange("p k n -> p (k n)"), t2[:, 64:64 + 2 * NG]))
            v.sem_inc(s_tidx, 1)
            link(v.tensor_tensor(ang, t1[:, NT:2 * NT].unsqueeze(2).broadcast_to([P, NT, HD // 2]),
                                 inv.unsqueeze(1).broadcast_to([P, NT, HD // 2]), ALU.mult))
            magic = 1.5 * 2.0 ** 23
            c1 = 6.28125
            c2 = float(np.float32(math.floor((2 * math.pi - c1) * 2.0 ** 21) / 2.0 ** 21))
            c3 = float(np.float32(2 * math.pi - c1 - c2))
            link(v.tensor_scalar(turn, ang, 1.0 / (2 * math.pi), magic, ALU.mult, ALU.add))
            link(v.tensor_scalar(turn, turn, magic, None, ALU.subtract))
            for cc in (c1, c2, c3):
                link(v.scalar_tensor_tensor(ang, turn, -cc, ang, ALU.mult, ALU.add))
            lim = 3.1415925
            link(v.tensor_scalar(ang, ang, -lim, lim, ALU.max, ALU.min))
            link(v.scalar_tensor_tensor(turn, ang, -1.0, ang, ALU.mult, ALU.max))
            link(v.tensor_scalar(turn, turn, -1.0, math.pi / 2, ALU.mult, ALU.add))
            v.sem_inc(s_red, 1)
            link(v.memset(eps_c, EPS))
            dve.wait_ge(s_itemg, 32 * NI)
            for s in range(NI):
                for k in range(2):
                    o = arena[:, s, k].rearrange("p (g o d) -> p g o d", g=G, o=BLOCK)
                    m = keep[:, 16 * s:16 * s + 16].unsqueeze(1).broadcast_to([P, G, BLOCK])
                    v.tensor_tensor(o, o, m.unsqueeze(3).broadcast_to([P, G, BLOCK, HD]), ALU.mult).then_inc(s_masked, 1)
            dve.wait_ge(s_trig, 2)
            dve.wait_ge(s_masked, 2 * NI)
            v.sem_inc(s_pre, 1)

            dve.wait_ge(s_x, 16)

            def a_slot(i, c):
                k = A_UN * i + c
                if valid(k, NT):
                    dve.wait_ge(s_l0, k + 1)
                    wait(dve, s_xt, k - 1)
                    wait(dve, s_xc, k - 1)
                    v.tensor_tensor(x1s[c % 2], psl[c % 2][:, 0:D], xall[:, k, :], ALU.add).then_inc(s_x1, 1)
                k = A_UN * i + c - 3
                b = (c - 3) % 2
                if valid(k, NT):
                    dve.wait_ge(s_sq, k + 1)
                    v.tensor_reduce(st[b][:, 0:HEADS], sq[b].rearrange("p (h d) -> p h d", d=HD), AX.X, ALU.add).then_inc(s_ss, 1)
                k = A_UN * i + c - 4
                b, r = (c - 4) % 2, (c - 4) % 4
                if valid(k, NT):
                    q4 = qg[b].rearrange("p (h e d) -> p h e d", e=2, d=HD // 2)
                    b4 = rb[b].rearrange("p (h e d) -> p h e d", e=2, d=HD // 2)
                    a4 = ra[b].rearrange("p (h e d) -> p h e d", e=2, d=HD // 2)
                    o4 = qkvr[r][:, 0:QK].rearrange("p (h e d) -> p h e d", e=2, d=HD // 2)
                    sn = sin[:, k, :].unsqueeze(1).broadcast_to([P, HEADS, HD // 2])
                    dve.wait_ge(s_qg, k + 1)
                    wait(dve, s_qr, 2 * k - 2)
                    for e in range(2):
                        v.tensor_tensor(b4[:, :, e], q4[:, :, 1 - e], sn, ALU.mult).then_inc(s_rb, 1)
                    dve.wait_ge(s_rb, 2 * k + 2)
                    dve.wait_ge(s_ra, k + 1)
                    wait(dve, s_scat[r], 16 * (i + (c - 8) // 4 + 1))
                    wait(dve, s_qt, k - 3)
                    v.tensor_tensor(o4[:, :, 0], a4[:, :, 0], b4[:, :, 0], ALU.subtract).then_inc(s_qr, 1)
                    v.tensor_tensor(o4[:, :, 1], a4[:, :, 1], b4[:, :, 1], ALU.add).then_inc(s_qr, 1)
                k = A_UN * i + c - 3
                b = (c - 3) % 2
                if valid(k, NT):
                    dve.wait_ge(s_st, k + 1)
                    v.reciprocal(st[b][:, 2 * HEADS:3 * HEADS], st[b][:, HEADS:2 * HEADS]).then_inc(s_rc, 1)
                    dve.wait_ge(s_rc, k + 1)
                    wait(dve, s_qg, k - 1)
                    v.tensor_tensor(qn[b].rearrange("p (h d) -> p h d", d=HD),
                                    psq[b][:, 0:QK].rearrange("p (h d) -> p h d", d=HD),
                                    st[b][:, 2 * HEADS:3 * HEADS].unsqueeze(2).broadcast_to([P, HEADS, HD]),
                                    ALU.mult).then_inc(s_qn, 1)

            for n in range(3 * A_UN):
                a_slot(n // A_UN, n % A_UN)
            with dve.Fori(3, NT // A_UN - 1) as i:
                for c in range(A_UN):
                    a_slot(i, c)
            for n in range(NT - A_UN, NT + 6):
                a_slot(n // A_UN, n % A_UN)

            for w in range(2 * NI):
                s, h = w // 2, w % 2
                dve.wait_ge(s_stage[w % 2], 16 * (w // 2 + 1))
                o = arena[:, s, 0].rearrange("p (g o d) -> p g o d", g=G, o=BLOCK)[:, :, 8 * h:8 * h + 8, :]
                v.tensor_tensor(o, o, stage[:, w % 2, :, 0:G * HD].rearrange("p o (g d) -> p g o d", g=G),
                                ALU.add).then_inc(s_addk, 1)

            def b_slot(i, c):
                U = 16 * i + c + 1
                b = (c + 1) % 2
                if valid(U, NU):
                    dve.wait_ge(s_mk, 2 * (4 * i + (c + 1) // 4) + 2)
                    wait(dve, s_e, U - 1)
                    wait_first(dve, s_s, GB * i + (c + 1) // 2 + 1, s_passed[2])
                    for q in range(2):
                        v.tensor_tensor_reduce(smx[b][:, q], pss[(c + 1) % 4][:, KEYS * q:KEYS * (q + 1)],
                                               msk[((c + 1) // 4) % 2][:, KEYS * q:KEYS * (q + 1)], -1.0, MASKED * 256,
                                               ALU.add, ALU.min, accum_out=nmax[b][:, q:q + 1]).then_inc(s_sm, 1)
                w = c % GB
                g, par = 2 * i + c // GB + 1, (c // GB + 1) % 2
                if valid(g, NG) and w >= 4:
                    dve.wait_ge(s_kvt, GB * g + w + 1)
                    wait(dve, s_pv, GB * (g - 1))
                    v.transpose(vkeys[:, par, :, HD * (w - 4):HD * (w - 3)], window_columns(pskv)).then_inc(s_vc, 1)
                if c % 4 == 0:
                    n, b = 4 * i + c // 4 - 1, (c // 4 - 1) % 2
                    if valid(n, NT):
                        dve.wait_ge(s_e, 4 * n + 4)
                        v.reciprocal(rinv[b], rsum[b]).then_inc(s_rl, 1)
                U = 16 * i + c
                b = c % 2
                if valid(U, NU) and b == 0:
                    dve.wait_ge(s_pt, U + 1)
                    wait(dve, s_pv, U - 1)
                    v.tensor_copy(pts[b].rearrange("p g k -> p (g k)"), pspt[:, :]).then_inc(s_pc[0], 1)
                if c % 4 == 0:
                    n, b = 4 * i + c // 4 - 1, (c // 4 - 1) % 2
                    if valid(n, NT):
                        dve.wait_ge(s_pv, 4 * n + 4)
                        dve.wait_ge(s_rl, n + 1)
                        wait(dve, s_ot, n - 1)
                        for e in range(2):
                            r = slice(64 * e, 64 * e + 64)
                            v.tensor_tensor(on[b][r].rearrange("p (g d) -> p g d", g=2 * G),
                                            pso[r].rearrange("p (g e d) -> p g e d", g=2 * G, e=2)[:, :, e],
                                            rinv[b][r].unsqueeze(2).broadcast_to([64, 2 * G, HD]), ALU.mult).then_inc(s_on, 1)
                if c % 4 == 0:
                    n, b = 4 * i + (c - 8) // 4, ((c - 8) // 4) % 2
                    if valid(n, NT):
                        dve.wait_ge(s_l2, n + 1)
                        wait(dve, s_out[b], 16 * (2 * i + ((c - 8) // 4 - 2) // 2 + 1))
                        v.scalar_tensor_tensor(x4[b], psw[1], t2[:, bass.ds(96 + n, 1)], x2[b], ALU.add, ALU.add).then_inc(s_x4, 1)
                if c % 4 == 1:
                    n, par = 4 * i + c // 4 + 1, (c // 4 + 1) % 2
                    if valid(n, NT):
                        def bound(q, k):
                            return bounds[:, bass.ds(2 * n + q, 1), k:k + 1].rearrange("p a k -> p (a k)")
                        wait(dve, s_mk, 2 * n)
                        for q in range(2):
                            v.tensor_scalar(mska[:, q], kappa, bound(q, 0), bound(q, 2), ALU.max, ALU.subtract).then_inc(s_ma, 1)
                        wait(dve, s_sm, 8 * n - 8)
                        dve.wait_ge(s_ma, 2 * n + 2)
                        for q in range(2):
                            v.scalar_tensor_tensor(msk[par][:, KEYS * q:KEYS * (q + 1)], kappa, bound(q, 1), mska[:, q],
                                                   ALU.min, ALU.subtract).then_inc(s_mk, 1)
                if c % 4 == 2:
                    n, b = 4 * i + (c - 6) // 4, ((c - 6) // 4) % 2
                    if valid(n, NT):
                        dve.wait_ge(s_wo, n + 1)
                        wait(dve, s_x4, n - 1)
                        wait(dve, s_l2, n - 1)
                        v.tensor_tensor(x2[b], psw[0], xall[:, bass.ds(n, 1), :].rearrange("p a d -> p (a d)"), ALU.add).then_inc(s_x2, 1)

            run_b(dve, b_slot)

        @block.scalar
        def _(act):
            a = nc.scalar
            act.wait_ge(s_red, 1)
            a.activation(sin[:, :, :], ang, ACT.Sin).then_inc(s_trig, 1)
            a.activation(cos[:, :, :], turn, ACT.Sin).then_inc(s_trig, 1)
            act.wait_ge(s_pre, 1)

            def a_slot(i, c):
                k = A_UN * i + c
                if valid(k, NT):
                    act.wait_ge(s_x1, k + 1)
                    a.copy(xall[:, k, :], x1s[c % 2]).then_inc(s_xc, 1)
                k = A_UN * i + c - 1
                b = (c - 1) % 2
                if valid(k, NT):
                    act.wait_ge(s_xt, k + 1)
                    wait(act, s_qkv, k - 1)
                    a.copy(x1t[b], psx[b][:, 0:D].rearrange("p (c t) -> p c t", c=2)).then_inc(s_xtc, 1)
                k = A_UN * i + c - 3
                b = (c - 3) % 2
                if valid(k, NT):
                    act.wait_ge(s_ss, k + 1)
                    wait(act, s_rc, k - 1)
                    a.activation(st[b][:, HEADS:2 * HEADS], st[b][:, 0:HEADS], ACT.Sqrt, bias=eps_c, scale=1.0 / HD).then_inc(s_st, 1)
                k = A_UN * i + c - 2
                b, r = (c - 2) % 2, (c - 2) % 4
                if valid(k, NT):
                    act.wait_ge(s_qkv, k + 1)
                    wait(act, s_ss, k - 1)
                    a.activation(sq[b], psq[b][:, 0:QK], ACT.Square).then_inc(s_sq, 1)
                    wait(act, s_scat[r], 16 * (i + (c - 6) // 4 + 1))
                    a.copy(qkvr[r][:, QK:QKV], psq[b][:, QK:QKV]).then_inc(s_v, 1)
                k = A_UN * i + c - 5
                b = (c - 5) % 2
                if valid(k, NT):
                    act.wait_ge(s_qt, k + 1)
                    a.copy(qt[:, k].rearrange("p b h t -> p h b t"),
                           psqt[b][:, 0:GSZ * P].rearrange("p (h b t) -> p h b t", h=GSZ, b=TB)).then_inc(s_qtc, 1)

            for n in range(3 * A_UN):
                a_slot(n // A_UN, n % A_UN)
            with act.Fori(3, NT // A_UN - 1) as i:
                for c in range(A_UN):
                    a_slot(i, c)
            for n in range(NT - A_UN, NT + 6):
                a_slot(n // A_UN, n % A_UN)

            act.wait_ge(s_pz, 2)

            def b_slot(i, c):
                w = c % GB
                g, par = 2 * i + c // GB + 1, (c // GB + 1) % 2
                if valid(g, NG) and w < 4:
                    act.wait_ge(s_kvt, GB * g + w + 1)
                    wait(act, s_kd[(par + 1) % 2], 256 * (i + 1))
                    a.copy(ka[:, w].rearrange("p (m o j) -> p m o j", m=2 * GB, o=4),
                           pskv[:, 0:4 * WPX].rearrange("p (o m) -> p o m", o=4)[:, :, 0:WP]
                           .rearrange("p o (m j) -> p m o j", j=JH)).then_inc(s_kc, 1)
                U = 16 * i + c
                b = c % 2
                if valid(U, NU) and b == 1:
                    act.wait_ge(s_pt, U + 1)
                    wait(act, s_pv, U - 1)
                    a.copy(pts[b].rearrange("p g k -> p (g k)"), pspt[:, :]).then_inc(s_pc[1], 1)
                U = 16 * i + c + 1
                b = (c + 1) % 2
                if valid(U, NU):
                    n, g = 4 * i + (c + 1) // 4, (c + 1) % G
                    act.wait_ge(s_sm, 2 * U + 2)
                    wait(act, s_pt, U - 1)
                    wait(act, s_rl, n - 1)
                    for q in range(2):
                        e = a.activation(prob[b][:, q].rearrange("p h (o j) -> p (h o) j", j=8)[:, :, 0:JH],
                                         smx[b][:, q].rearrange("p (o j) -> p o j", j=JH), ACT.Exp,
                                         bias=nmax[b][:, q:q + 1], scale=-1.0,
                                         accum_out=rsum[((c + 1) // 4) % 2][:, G * q + g:G * q + g + 1])
                    e.then_inc(s_e, 1)
                if c % 4 == 1:
                    n, b = 4 * i + (c - 5) // 4, ((c - 5) // 4) % 2
                    if valid(n, NT):
                        act.wait_ge(s_ot, n + 1)
                        wait(act, s_wo, n - 1)
                        a.copy(ot[b], psot.rearrange("p (b h t) -> p h b t", b=TB, h=GSZ)).then_inc(s_oc, 1)

            run_b(act, b_slot)

        @block.tensor
        def _(pe):
            mm = nc.tensor.matmul
            pe.wait_ge(s_wsubj, 48)
            for s in range(SUBJ):
                last = mm(ps[6][0:T, T * s:T * (s + 1)], wsubj[:, 1, s], wsubj[:, 2, s], start=True, stop=True)
            last.then_inc(s_w23p, 1)
            pe.wait_ge(s_pairs, 1)
            for m, bank in ((later, ps[0]), (same, ps[1])):
                for s in range(NI):
                    for r in range(NI):
                        last = mm(bank[:, 16 * s:16 * s + 16], m[:, r].rearrange("p (b s) -> p s b", s=NI)[:, s],
                                  cov[:, 16 * r:16 * r + 16], start=(r == 0), stop=(r == NI - 1))
            last.then_inc(s_cnt, 1)
            pe.wait_ge(s_m, 80)
            nc.tensor.transpose(ps[2][:, 0:P], m1, ident)
            nc.tensor.transpose(ps[3][:, 0:P], m2, ident).then_inc(s_mt, 1)
            pe.wait_ge(s_wts, 32)
            pe.wait_ge(s_x, 16)
            pe.wait_ge(s_tidx, 1)

            def a_slot(i, c):
                k = A_UN * i + c
                b = c % 2
                if valid(k, NT):
                    pe.wait_ge(s_wbd, k + 1)
                    wait(pe, s_x1, k - 1)
                    mm(psl[b][:, 0:D], wbd[b], xall[:, k, :], start=True, stop=True).then_inc(s_l0, 1)
                k = A_UN * i + c - 1
                b = (c - 1) % 2
                if valid(k, NT):
                    pe.wait_ge(s_x1, k + 1)
                    wait(pe, s_xtc, k - 1)
                    nc.tensor.transpose(psx[b][:, 0:P], x1s[b][:, 0:P], ident)
                    nc.tensor.transpose(psx[b][:, P:2 * P], x1s[b][:, P:2 * P], ident).then_inc(s_xt, 1)
                k = A_UN * i + c - 2
                b = (c - 2) % 2
                if valid(k, NT):
                    pe.wait_ge(s_xtc, k + 1)
                    wait(pe, s_qn, k - 1)
                    wait(pe, s_v, k - 1)
                    for d in range(2):
                        last = mm(psq[b][:, :], x1t[b][:, d], wqkv_sb[:, d, :], start=(d == 0), stop=(d == 1))
                    last.then_inc(s_qkv, 1)
                k = A_UN * i + c - 5
                b, r = (c - 5) % 2, (c - 5) % 4
                if valid(k, NT):
                    pe.wait_ge(s_qr, 2 * k + 2)
                    wait(pe, s_qtc, k - 1)
                    q = qkvr[r][:, 0:H * HD].rearrange("p (h e) -> p h e", h=GSZ)
                    for h in range(GSZ):
                        last = nc.tensor.transpose(psqt[b][:, P * h:P * (h + 1)], q[:, h], ident)
                    last.then_inc(s_qt, 1)

            for n in range(3 * A_UN):
                a_slot(n // A_UN, n % A_UN)
            with pe.Fori(3, NT // A_UN - 1) as i:
                for c in range(A_UN):
                    a_slot(i, c)
            for n in range(NT - A_UN, NT + 6):
                a_slot(n // A_UN, n % A_UN)

            pe.wait_ge(s_qtc, NT)

            def keys_of(r, q, bb):
                return ktr[r:r + HD, q, 2 * bb:2 * bb + 2]

            def b_slot(i, c):
                if c % 2 == 0:
                    V = GB * i + c // 2 + 1
                    if valid(V, NU // 2):
                        q = ((c + 2) // GB) % 2
                        g8 = 2 * i + (c + 2) // GB
                        pe.wait_ge(s_qs, g8 + 1)
                        pe.wait_ge(s_kd[q], 256 * (i + (c + 2) // 16 + 1))
                        wait(pe, s_sm, 4 * (V - 1))
                        for k in range(2):
                            for u in range(2):
                                for e in range(2):
                                    r = HD * ((c + 2 + u) % G)
                                    bb = TB * (((c + 2) % GB) // 4) + 2 * k + e
                                    last = mm(pss[(c + 2 + u) % 4][64 * e:64 * e + 64, KEYS * k:KEYS * (k + 1)],
                                              qs[q][r:r + HD, 64 * bb:64 * bb + 64],
                                              keys_of(r, q, bb), start=True, stop=True)
                        last.then_inc(s_s, 1)
                w = c % GB
                g8, par = 2 * i + c // GB + 1, (c // GB + 1) % 2
                if valid(g8, NG):
                    if w == 0:
                        pe.wait_ge(s_win[par], 32 * (i + (c // GB + 1) // 2 + 1))
                    if w == 0:
                        wait(pe, s_vc, 4 * g8)
                    elif w < 5:
                        pe.wait_ge(s_kc, 4 * g8 + w)
                    else:
                        pe.wait_ge(s_vc, 4 * g8 + w - 4)
                    for o in range(4):
                        first = BLOCK * HD * (w % 4) + P * o
                        src = arena[0:WPX, par, w // 4, first:first + P]
                        last = nc.tensor.transpose(pskv[:, WPX * o:WPX * (o + 1)], src, ident[0:WPX, 0:WPX])
                    last.then_inc(s_kvt, 1)
                U = 16 * i + c
                b = c % 2
                if valid(U, NU):
                    pe.wait_ge(s_e, U + 1)
                    wait(pe, s_pc[1 - b], GB * i + (c + 1) // 2)
                    for k in range(4):
                        last = nc.tensor.transpose(pspt[:, P * k:P * (k + 1)], prob[b][:, k // 2, k % 2], ident)
                    last.then_inc(s_pt, 1)
                U = 16 * i + c - 1
                b, q = (c - 1) % 2, ((c - 1) // GB) % 2
                if valid(U, NU):
                    n, g = 4 * i + (c - 1) // 4, (c - 1) % G
                    pe.wait_ge(s_pc[b], GB * i + (c - 1) // 2 + 1)
                    pe.wait_ge(s_vc, 4 * (2 * i + (c - 1) // GB) + 4)
                    if g == 0:
                        wait(pe, s_on, 2 * n)
                    for k in range(2):
                        col = 2 * HD * (G * k + g)
                        bb = TB * (((c - 1) % GB) // 4) + 2 * k
                        for h in range(2):
                            last = mm(pso[:, col:col + 2 * HD].rearrange("p (e d) -> p e d", e=2), pts[b][:, 2 * k + h],
                                      vkeys[:, q, 2 * bb + h:2 * bb + h + 3:2, HD * g:HD * (g + 1)], start=(h == 0), stop=(h == 1))
                    last.then_inc(s_pv, 1)
                if c % 4 == 1:
                    n, b = 4 * i + (c - 5) // 4, ((c - 5) // 4) % 2
                    if valid(n, NT):
                        pe.wait_ge(s_on, 2 * n + 2)
                        wait(pe, s_x4, n)
                        for k in range(2):
                            last = nc.tensor.transpose(psot[:, P * k:P * (k + 1)], on[b][:, P * k:P * (k + 1)], ident)
                        last.then_inc(s_ot, 1)
                if c % 4 == 2:
                    n, b = 4 * i + (c - 6) // 4, ((c - 6) // 4) % 2
                    if valid(n, NT):
                        pe.wait_ge(s_oc, n + 1)
                        for h in range(GSZ):
                            last = mm(psw[0], ot[b][:, h].rearrange("p b t -> p (b t)"), wo_sb[:, h, :], start=(h == 0), stop=(h == 1))
                        last.then_inc(s_wo, 1)
                if c % 4 == 3:
                    n, b = 4 * i + (c - 7) // 4, ((c - 7) // 4) % 2
                    if valid(n, NT):
                        pe.wait_ge(s_x2, n + 1)
                        pe.wait_ge(s_w23, n + 1)
                        mm(psw[1], wbd2[b], x2[b], start=True, stop=True).then_inc(s_l2, 1)

            run_b(pe, b_slot)


def kernel(**inputs):
    import concourse.bacc as _bacc
    from concourse import mybir as _mybir
    from concourse.bass_utils import run_bass_kernel_spmd as _run

    a = {k: np.ascontiguousarray(v) for k, v in inputs.items()}
    wqkv = np.concatenate([a["L1_cond_Wq"].reshape(G, GSZ, HD, D).transpose(1, 0, 2, 3).reshape(H * HD, D), a["L1_cond_Wk"], a["L1_cond_Wv"]], 0).T
    wqkv = wqkv.reshape(2, P, QKV).transpose(1, 0, 2)
    wo = a["L1_cond_Wo"].T.reshape(G, GSZ, HD, D).transpose(0, 2, 1, 3).reshape(P, GSZ, D)
    arrays = {
        "x": a["x"], "conditions": a["itok_B_1_198"], "tables": a["itok_Bx257_0_4111"], "kv_lens": a["itok_B_37_3939"],
        "subjects": a["itok_B_0_7"], "bias": a["fside_8xS_0"], "w0": a["L0_cond_weights"], "w2": a["L2_cond_weights"],
        "w2t": a["L2_cond_weights"].transpose(0, 2, 1),
        "w3": a["L3_cond_weights"], "wqkv": wqkv, "wo": wo, "q_scale": a["L1_cond_q_norm_scale"],
        "k_scale": a["L1_cond_k_norm_scale"], "k_cache": a["L1_cond_k_blocks"], "v_cache": a["L1_cond_v_blocks"],
        "consts": constants(),
    }
    arrays = {k: np.ascontiguousarray(v) for k, v in arrays.items()}
    nc = _bacc.Bacc("TRN2", target_bir_lowering=False, num_devices=1)
    args = [nc.dram_tensor(k, v.shape, _mybir.dt.from_np(v.dtype), kind="ExternalInput").ap() for k, v in arrays.items()]
    out = nc.dram_tensor("out", (B, T, D), F32, kind="ExternalOutput").ap()
    build(nc, *args, out)
    r = _run(nc, [arrays], core_ids=[0])
    return r.results[0]["out"]
```

```python
import math
from contextlib import ExitStack

import numpy as np
import concourse.bass as bass
from concourse import mybir

F32 = mybir.dt.float32
I32 = mybir.dt.int32
BF16 = mybir.dt.bfloat16
ALU = mybir.AluOpType
ACT = mybir.ActivationFunctionType
AX = mybir.AxisListType

P = 128
B, T, D = 128, 32, 256
H, G, HD = 8, 4, 32
GSZ = H // G
BLOCK, WINDOW = 16, 128
SUBJ = 8
EPS = 1e-6
TB = P // T
NT = B // TB
SPAN = WINDOW // BLOCK
NI = 3
SLOTS = SPAN + NI
JH = (SLOTS + 1) // 2
WS = 2 * JH
GB = 8
NG = B // GB
WP = GB * WS
WPX = (2 * GB - 1) * JH + 8
KEYS = WS * BLOCK
BE = G * BLOCK * HD
FAR = 1.0e6
MASKED = 2.0 ** 100
HEADS = H + G
QK = HEADS * HD
QKV = QK + G * HD

C_ID, C_BM, C_KAP, C_INV, C_IOTA, C_ITEM = 0, 128, 132, 132 + KEYS, 148 + KEYS, 148 + KEYS + 388
C_END = C_ITEM + NI


def constants():
    c = np.zeros((P, C_END), np.float32)
    p = np.arange(P)
    c[:, C_ID:C_ID + P] = np.eye(P)
    c[:, C_BM:C_BM + TB] = (p[:, None] // T == np.arange(TB))
    h, r, o, j = np.meshgrid(np.arange(2), np.arange(4), np.arange(4), np.arange(JH), indexing="ij")
    c[:, C_KAP:C_KAP + KEYS] = MASKED * ((JH * h + j) * BLOCK + 4 * o + r).reshape(-1)
    half = HD // 2
    c[:, C_INV:C_INV + half] = np.float32(1.0) / np.float32(10000.0) ** (np.arange(half, dtype=np.float32) / np.float32(half))
    c[:, C_IOTA:C_IOTA + 388] = np.arange(388)
    c[:, C_ITEM:C_ITEM + NI] = NI * p[:, None] + np.arange(NI)
    return c


def valid(index, count):
    return not isinstance(index, int) or 0 <= index < count


def wait(eng, sem, value):
    if not isinstance(value, int) or value > 0:
        eng.wait_ge(sem, value)


def wait_first(eng, sem, value, passed):
    wait(eng, sem, value)
    if not isinstance(value, int):
        eng.sem_inc(passed, 1)


def build(nc, x, conditions, tables, kv_lens, subjects, bias, w0, w2, w2t, w3, wqkv, wo, q_scale, k_scale,
          k_cache, v_cache, consts, out):
    NBLK = tables.shape[1]
    NCACHE = k_cache.shape[0]
    ctx = ExitStack()
    with ctx:
        def sb(name, shape, dt=F32):
            return ctx.enter_context(nc.sbuf_tensor(name, shape, dt))

        def sem(name):
            return ctx.enter_context(nc.semaphore(name))

        d_w = [nc.dram_tensor(f"d_w{k}", (B, T * T), F32).ap() for k in range(2)]
        d_w23 = nc.dram_tensor("d_w23", (SUBJ, T * T), F32).ap()
        d_item = nc.dram_tensor("d_item", (B, NI), F32).ap()
        d_m1 = nc.dram_tensor("d_m1", (P, P), F32).ap()
        d_m2 = nc.dram_tensor("d_m2", (P, P), F32).ap()
        d_win = nc.dram_tensor("d_win", (2, B, WS), F32).ap()
        new_rows = nc.dram_tensor("new_rows", (B * NI * BLOCK, 2 * G * HD), F32).ap()
        patched = [nc.dram_tensor(f"patched_{k}", (B * NI, BE), F32).ap() for k in "kv"]

        xall = sb("xall", [P, NT, D])
        qt = sb("qt", [P, NT, TB, GSZ, T])
        wc = [sb(f"wc{k}", [P, NT, T]) for k in range(2)]
        xmix = sb("xmix", [P, T * T])
        wsubj = sb("wsubj", [T, 4, SUBJ, T])
        wqkv_sb = sb("wqkv_sb", [P, 2, QKV])
        wo_sb = sb("wo_sb", [P, GSZ, D])
        cst = sb("cst", [P, C_END])
        gain = sb("gain", [P, HEADS, HD])
        scales = sb("scales", [P, 2, HD])
        cos = sb("cos", [P, NT, HD // 2])
        sin = sb("sin", [P, NT, 2, HD // 2])
        t1 = sb("t1", [P, P])
        t2 = sb("t2", [P, P])
        toki = sb("toki", [P, NT], I32)
        wini = sb("wini", [P, 2, NG], I32)
        bounds = sb("bounds", [P, B // 2, 3])
        rowi = sb("rowi", [P, 4], I32)
        blki = sb("blki", [P, 2, 2], I32)
        arena = sb("arena", [P, 4, 2, BE])
        vkeys = arena[:, 2].rearrange("p a (m e) -> p a m e", m=2 * GB)
        ktr = arena[:, 3, :, 0:WP * BLOCK]
        ktr = ktr.rearrange("p a (r m e) -> p a m r e", r=4, m=2 * GB)

        ident = cst[:, C_ID:C_ID + P]
        bmask = cst[:, C_BM:C_BM + TB]
        kappa = cst[:, C_KAP:C_KAP + KEYS]
        inv = cst[:, C_INV:C_INV + HD // 2]

        def iota(n, first=0):
            return cst[:, C_IOTA + first:C_IOTA + first + n]

        WORK = 10240
        work = sb("work", [P, WORK])
        small = sb("small", [P, 512])
        smalli = sb("smalli", [P, 16], I32)
        at = [0]
        stage = [a.rearrange("p (o e) -> p o e", o=BLOCK) for a in
                 (arena[:, 3].rearrange("p a e -> p (a e)"), work[:, 0:2 * BE], work[:, 2 * BE:4 * BE])]

        def cut(n):
            a = work[:, at[0]:at[0] + n]
            at[0] += n
            assert at[0] <= WORK, at[0]
            return a

        tabs = wc[1][:, :, :].rearrange("p n d -> p (n d)")
        tab_f, tab_i, pick = tabs[:, 0:NBLK], tabs[:, NBLK:2 * NBLK].bitcast(I32), tabs[:, 2 * NBLK:3 * NBLK]
        pre = arena[:, 3].rearrange("p a e -> p (a e)")
        pat = [0]

        def pcut(n):
            a = pre[:, pat[0]:pat[0] + n]
            pat[0] += n
            assert pat[0] <= 2 * BE, pat[0]
            return a

        zero_row = pcut(2 * G * HD)
        item_row = pcut(B * NI)
        same = pcut(NI * B * NI // 2).bitcast(BF16).rearrange("p (s i) -> p s i", s=NI)
        later = pcut(NI * B * NI // 2).bitcast(BF16).rearrange("p (s i) -> p s i", s=NI)
        spread = pcut(T * BLOCK)
        chosen = pcut(B * NI)
        last_num = pcut(B * NI)
        ones = pcut(P // 2).bitcast(BF16)
        cov = pcut(NI * BLOCK // 2).bitcast(BF16)
        m1 = pcut(P)
        m2 = pcut(P)
        pack = pcut(32 + 32 + 64 + 64 + 2 * WS)
        p_tok, p_pos = pack[:, 0:32], pack[:, 32:64]
        p_up = pack[:, 64:128].rearrange("p (h t) -> p h t", h=GSZ)
        p_low = pack[:, 128:192].rearrange("p (h t) -> p h t", h=GSZ)
        p_win = pack[:, 192:192 + 2 * WS].rearrange("p (k j) -> p k j", k=2)
        biasg = pcut(T)
        ang, turn = sin[:, :, 1], cos[:, :, :]
        wbd = [cut(P) for _ in range(2)]
        x1s = [cut(D) for _ in range(2)]
        x1t = [cut(D).rearrange("p (c t) -> p c t", c=2) for _ in range(2)]
        sq = [cut(QK) for _ in range(2)]
        qn = [cut(QK) for _ in range(2)]
        qg = [cut(QK) for _ in range(2)]
        ra = [cut(QK) for _ in range(2)]
        rb = [cut(QK) for _ in range(2)]
        qkvr = [cut(QKV) for _ in range(4)]
        st = [cut(3 * HEADS) for _ in range(2)]
        at[0] = 0
        qs = [cut(GB * GSZ * T) for _ in range(2)]
        msk = [cut(2 * KEYS) for _ in range(2)]
        mska = cut(2 * KEYS).rearrange("p (q k) -> p q k", q=2)
        smx = [cut(2 * KEYS).rearrange("p (q k) -> p q k", q=2) for _ in range(2)]
        prob = [cut(4 * P).rearrange("p (q h k) -> p q h k", q=2, h=2) for _ in range(2)]
        pts = [cut(4 * P).rearrange("p (g k) -> p g k", g=4) for _ in range(2)]
        on = [cut(2 * P) for _ in range(2)]
        ot = [cut(GSZ * P).rearrange("p (h b t) -> p h b t", h=GSZ, b=TB) for _ in range(2)]
        wbd2 = [cut(P) for _ in range(2)]
        x2 = [cut(D) for _ in range(2)]
        x4 = [cut(D) for _ in range(2)]
        ka = cut(G * 4 * WP).rearrange("p (g k) -> p g k", g=G)
        nmax = [cut(2) for _ in range(2)]
        rsum = [cut(2 * G) for _ in range(2)]
        rinv = [cut(2 * G) for _ in range(2)]

        kv_i, f_i, s_i, sub_i, con_i = (smalli[:, k:k + 1] for k in range(5))
        blk_i = smalli[:, 8:8 + NI]
        kv_f, f_f, s_f, f32_f, low_f = (small[:, k:k + 1] for k in range(5))
        eps_c = small[:, 5:6]
        sidx = small[:, 8:8 + SLOTS]
        blk = small[:, 24:24 + SLOTS]
        rep = small[:, 40:40 + SLOTS]
        hit = small[:, 56:56 + SLOTS]
        base = small[:, 72:72 + NI]
        fmask = small[:, 80:96]
        wins = small[:, 144:192]
        keep = small[:, 192:240]
        cell = small[:, 240:288]
        ft = small[:, 288:320]
        tmp48 = small[:, 320:368]
        miss = small[:, 368:368 + SLOTS]

        ps = [ctx.enter_context(nc.psum_tensor(f"ps{k}", [P, 512], F32)) for k in range(8)]

        s_kv, s_tab, s_cs, s_idx, s_cst = sem("kv_loaded"), sem("tables_loaded"), sem("choices_loaded"), sem("items_stored"), sem("consts_loaded")
        s_x = [sem(f"x_loaded{k}") for k in range(3)]
        s_wts, s_scl = sem("weights_loaded"), sem("scales_loaded")
        s_mixg = [sem(f"mix_gathered{k}") for k in range(2)]
        s_mixd = [sem(f"mix_stored{k}") for k in range(2)]
        s_mix = [sem(f"mix_loaded{k}") for k in range(2)]
        s_biasg = sem("biases_gathered")
        s_itemrow, s_blk, s_blki = sem("item_row_loaded"), sem("blocks_found"), sem("block_indices")
        s_itemg = sem("item_blocks_gathered")
        s_zero, s_zeroed, s_ones = sem("zero_row"), sem("new_rows_zeroed"), sem("ones_ready")
        s_pairs, s_cnt = sem("item_pairs"), sem("later_counts")
        s_counted = sem("counts_read")
        s_early, s_earlyd, s_m1 = sem("positions_ready"), sem("positions_stored"), sem("positions_loaded")
        s_pack, s_packd, s_m = sem("pack_ready"), sem("pack_stored"), sem("matrices_loaded")
        s_mz, s_mt, s_tidx = sem("matrix_cleared"), sem("matrices_transposed"), sem("indices_ready")
        s_trig, s_red = sem("angles_done"), sem("angles_reduced")
        s_dve = sem("vector_step")
        s_wsubj, s_w23p, s_w23s, s_w23d = sem("mixes_loaded_by_subject"), sem("mix_products"), sem("mixes_combined"), sem("combined_mixes_stored")
        s_gain, s_masked = sem("gain_ready"), sem("old_rows_masked")
        s_wbd, s_l0, s_x1, s_xc, s_xt, s_xtc, s_qkv = (sem(n) for n in ("mix0_ready", "mix0_done", "x1_ready", "x1_kept", "x1_transposed", "x1t_ready", "qkv_done"))
        s_sq, s_v, s_ss, s_st, s_rc, s_qn, s_qg, s_ra, s_rb, s_qr, s_qt, s_qtc = (sem(n) for n in (
            "squares", "v_copied", "square_sums", "norms", "norm_recips", "normed", "gained", "rope_cos", "rope_sin",
            "qk_ready", "q_transposed", "qt_ready"))
        s_scat = [sem(f"rows_scattered{k}") for k in range(4)]
        s_stage = [sem(f"new_rows_loaded{k}") for k in range(NI)]
        s_addk, s_addv = sem("k_and_half_v_patched"), sem("other_half_v_patched")
        s_patched = [sem(f"patched_stored{k}") for k in range(NI)]
        s_old = [sem(f"old_blocks_loaded{k}") for k in range(2)]
        s_win = [sem(f"window_loaded{k}") for k in range(2)]
        s_kvt, s_kc, s_vc, s_qs = sem("window_transposed"), sem("keys_ready"), sem("values_ready"), sem("queries_staged")
        s_kd = [sem(f"keys_moved{k}") for k in range(2)]
        s_passed = [sem("gpsimd_passed"), sem("sync_passed"), sem("vector_passed")]
        s_ma, s_mk = sem("mask_parts"), sem("mask_ready")
        s_s, s_sm, s_e, s_pt, s_pv = (sem(n) for n in (
            "scores", "masked_scores", "probs", "probs_transposed", "pv_done"))
        s_rl, s_on, s_ot, s_oc, s_wo, s_w23 = (sem(n) for n in ("sum_recips", "o_normed", "o_transposed", "ot_ready", "wo_done", "mix23_ready"))
        s_x2, s_l2, s_x4 = (sem(n) for n in ("x2_ready", "mix23_done", "x4_ready"))
        s_out = [sem(f"out_stored{k}") for k in range(2)]
        s_pc = [sem(f"probs_t_ready{k}") for k in range(2)]
        s_pz, s_ri, s_bi = sem("probs_cleared"), sem("row_indices"), sem("window_indices")

        psl, psx, psq, psqt = ps[0:2], ps[2], ps[3:7], ps[7]
        pss, pspt, pskv = ps[0:4], ps[4], ps[5]
        pso, psot = ps[6], ps[7][:, 0:256]
        psw = [ps[7][:, 256:512], ps[7][:, 0:256]]

        xv = x.rearrange("(n b) c t -> (b c) n t", b=TB)
        outv = out.rearrange("(n b) c t -> n (b c) t", b=TB)
        mixv = [d.rearrange("(n b) (c d) -> (b c) n d", b=TB, c=T) for d in d_w]
        rowsv = new_rows.rearrange("(b s o) e -> s b o e", s=NI, o=BLOCK)
        patchedv = [d.rearrange("(b s) e -> s b e", s=NI) for d in patched]
        cachev = [c.rearrange("n g o d -> n (g o d)") for c in (k_cache, v_cache)]

        A_UN = 4
        NU = NG * GB

        block = ctx.enter_context(nc.Block())

        def add_rows(eng, s, k, h0, h1):
            o = arena[:, s, k].rearrange("p (g o d) -> p g o d", g=G, o=BLOCK)[:, h0:h1]
            n = stage[s][:, :, (G * k + h0) * HD:(G * k + h1) * HD].rearrange("p o (g d) -> p g o d", d=HD)
            return eng.tensor_tensor(o, o, n, ALU.add)

        def window_bank(i, c):
            first_group = isinstance(i, int) and i == -1 and c < 15
            return (pspt if first_group and c % 2 else pskv), first_group

        def run_b(eng, slot):
            for i in (-1, 0):
                for c in range(16):
                    slot(i, c)
            with eng.Fori(1, NG // 2 - 1) as i:
                for c in range(16):
                    slot(i, c)
            for i in (NG // 2 - 1, NG // 2):
                for c in range(16):
                    slot(i, c)

        def ktr_rows(par, g, r):
            return arena[HD * g:HD * (g + 1), 3, par, 4 * WP * r:4 * WP * (r + 1)]

        def window_columns(bank):
            a = bank[:, 0:4 * WPX].rearrange("p (o m) -> p o m", o=4)
            lap = a[:, :, 0:8].unsqueeze(1).broadcast_to([P, 2 * GB, 4, 8])
            return bass.AP(tensor=lap.tensor, offset=lap.offset, ap=[lap.ap[0], [JH, 2 * GB], lap.ap[2], lap.ap[3]])

        @block.sync
        def _(sp):
            sp.dma_start(kv_i, kv_lens.unsqueeze(1)).then_inc(s_kv, 16)
            sp.dma_start(con_i, conditions.unsqueeze(1)).then_inc(s_cs, 16)
            sp.dma_start(sub_i, subjects.unsqueeze(1)).then_inc(s_cs, 16)
            sp.dma_start(tab_i, tables).then_inc(s_tab, 16)
            sp.wait_ge(s_early, 1)
            sp.dma_start(d_m1[0:32, :].rearrange("n (b t) -> (n b) t", b=TB), p_pos).then_inc(s_earlyd, 16)
            sp.dma_start(d_m1[32:96, :].rearrange("n (b t) -> (n b) t", b=2), pack[:, 64:128]).then_inc(s_earlyd, 16)
            sp.wait_ge(s_biasg, 16)
            sp.dma_start(d_m1[96:128, :].rearrange("n (b t) -> (n b) t", b=TB), biasg).then_inc(s_earlyd, 16)
            sp.wait_ge(s_blk, 1)
            sp.dma_start(d_item, blk[:, SPAN:SLOTS]).then_inc(s_idx, 16)
            sp.wait_ge(s_earlyd, 48)
            sp.dma_start(m1, d_m1).then_inc(s_m1, 16)
            sp.wait_ge(s_idx, 16)
            sp.dma_start(item_row, d_item.rearrange("b s -> (b s)").partition_broadcast(P)).then_inc(s_itemrow, 16)
            sp.wait_ge(s_mixg[0], 16)
            sp.dma_start(d_w[0], xmix[:, :]).then_inc(s_mixd[0], 16)
            sp.wait_ge(s_mixd[0], 16)
            sp.dma_start(wc[0][:, :, :], mixv[0]).then_inc(s_mix[0], 16)
            sp.wait_ge(s_w23s, 2)
            sp.dma_start(d_w23.rearrange("s (c d) -> c s d", c=T), wsubj[:, 3]).then_inc(s_w23d, 16)
            sp.wait_ge(s_pack, 1)
            sp.dma_start(d_m2[0:32, :].rearrange("n (b t) -> (n b) t", b=TB), p_tok).then_inc(s_packd, 16)
            sp.dma_start(d_m2[32:96, :].rearrange("n (b t) -> (n b) t", b=2), pack[:, 128:192]).then_inc(s_packd, 16)
            for k in range(2):
                sp.dma_start(d_win[k], p_win[:, k]).then_inc(s_packd, 16)
            sp.wait_ge(s_packd, 64)
            sp.wait_ge(s_mz, 1)
            sp.dma_start(m2[0:96, :], d_m2[0:96, :]).then_inc(s_m, 16)
            for k in range(2):
                sp.dma_start(m2[96 + NG * k:96 + NG * (k + 1), 0:WP],
                             d_win[k].rearrange("(n b) j -> n (b j)", b=GB)).then_inc(s_m, 16)
            sp.dma_start(rowsv[NI - 1], zero_row.unsqueeze(1).broadcast_to([P, BLOCK, 2 * G * HD])).then_inc(s_zeroed, 16)
            sp.dma_start(xall[:, NT // 4:NT // 2, :], xv[:, NT // 4:NT // 2, :]).then_inc(s_x[1], 16)
            sp.dma_start(xall[:, NT // 2:NT, :], xv[:, NT // 2:NT, :]).then_inc(s_x[2], 16)
            sp.wait_ge(s_mixg[1], 16)
            sp.dma_start(d_w[1], xmix[:, :]).then_inc(s_mixd[1], 16)
            sp.wait_ge(s_mixd[1], 16)
            sp.dma_start(wc[1][:, :, :], mixv[1]).then_inc(s_mix[1], 16)
            for k in range(4):
                sp.wait_ge(s_scat[k], 16 * (NT // 4))
            sp.wait_ge(s_qtc, NT)
            for s in range(NI - 1):
                sp.dma_start(stage[s], rowsv[s]).then_inc(s_stage[s], 16)
            for s in range(NI):
                sp.wait_ge(s_addk, 2 * s + 1)
                sp.dma_start(patchedv[0][s], arena[:, s, 0]).then_inc(s_patched[s], 16)
                sp.wait_ge(s_addk, 2 * s + 2)
                sp.wait_ge(s_addv, s + 1)
                sp.dma_start(patchedv[1][s], arena[:, s, 1]).then_inc(s_patched[s], 16)
                if s == 0:
                    sp.dma_start(stage[NI - 1], rowsv[NI - 1]).then_inc(s_stage[NI - 1], 16)
            def b_slot(i, c):
                w = (c + 1) % GB - 1
                g, par = 2 * i + (c + 1) // GB + 1, ((c + 1) // GB + 1) % 2
                if valid(g, NG) and 0 <= w < G:
                    wait_first(sp, s_kc, 4 * g + w + 1, s_passed[1])
                    wait(sp, s_s, G * (g - 1))
                    for r in range(4):
                        sp.dma_start(ktr_rows(par, w, r), ka[HD * r:HD * (r + 1), w]).then_inc(s_kd[par], 16)
                if c % 4 == 1:
                    n, b = 4 * i + (c - 9) // 4, ((c - 9) // 4) % 2
                    if valid(n, NT):
                        wait_first(sp, s_x4, n + 1, s_passed[1])
                        sp.dma_start(outv[n], x4[b]).then_inc(s_out[b], 16)
            run_b(sp, b_slot)
            for k in range(2):
                sp.wait_ge(s_out[k], 16 * (NT // 2))

        @block.gpsimd
        def _(pool):
            pool.wait_ge(s_cs, 32)
            pool.indirect_dma_start(out=biasg, out_offset=None, in_=bias,
                                    in_offset=bass.IndirectOffsetOnAxis(ap=sub_i, axis=0),
                                    bounds_check=SUBJ - 1, oob_is_err=False).then_inc(s_biasg, 16)
            pool.indirect_dma_start(out=xmix[:, :], out_offset=None, in_=w0.rearrange("n c d -> n (c d)"),
                                    in_offset=bass.IndirectOffsetOnAxis(ap=con_i, axis=0),
                                    bounds_check=w0.shape[0] - 1, oob_is_err=False).then_inc(s_mixg[0], 16)
            pool.memset(m2, 0.0).then_inc(s_mz, 1)
            pool.memset(zero_row, 0.0).then_inc(s_zero, 1)
            pool.memset(ones, 1.0).then_inc(s_ones, 1)

            def expand(dst, src, sm):
                nc.gpsimd.tensor_tensor(dst.rearrange("p (b d) -> p b d", b=TB),
                                        src.unsqueeze(1).broadcast_to([P, TB, T]),
                                        bmask.unsqueeze(2).broadcast_to([P, TB, T]), ALU.mult).then_inc(sm, 1)

            def a_slot(i, c):
                k = A_UN * i + c + 1
                if valid(k, NT):
                    wait(pool, s_l0, k - 1)
                    expand(wbd[(c + 1) % 2], wc[0][:, k, :], s_wbd)
                k = A_UN * i + c - 4
                if valid(k, NT):
                    b = (c - 4) % 2
                    pool.wait_ge(s_qn, k + 1)
                    wait(pool, s_rb, k - 1)
                    wait(pool, s_ra, k - 1)
                    nc.gpsimd.tensor_tensor(qg[b], qn[b], gain[:, :, :].rearrange("p h d -> p (h d)"), ALU.mult).then_inc(s_qg, 1)
                k = A_UN * i + c - 6
                if valid(k, NT):
                    r = (c - 6) % 4
                    pool.wait_ge(s_qr, k + 1)
                    pool.wait_ge(s_v, k + 1)
                    if isinstance(k, int) and k == 0:
                        pool.wait_ge(s_zeroed, 48)
                        pool.wait_ge(s_tidx, 1)
                    wait(pool, s_scat[r], 16 * (i + (c - 10) // 4 + 1))
                    nc.gpsimd.tensor_copy(rowi[:, r:r + 1], toki[:, bass.ds(k, 1)]).then_inc(s_ri, 1)
                    wait_first(pool, s_ri, k + 1, s_passed[0])
                    pool.indirect_dma_start(out=new_rows,
                                            out_offset=bass.IndirectOffsetOnAxis(ap=rowi[:, r:r + 1], axis=0),
                                            in_=qkvr[r][:, H * HD:QKV], in_offset=None,
                                            bounds_check=B * NI * BLOCK - 1, oob_is_err=False).then_inc(s_scat[r], 16)
                    if isinstance(k, int) and k == 2 * NI - 1:
                        pool.wait_ge(s_w23d, 16)
                        pool.wait_ge(s_mixd[0], 16)
                        pool.indirect_dma_start(out=xmix[:, :], out_offset=None, in_=d_w23,
                                                in_offset=bass.IndirectOffsetOnAxis(ap=sub_i, axis=0),
                                                bounds_check=SUBJ - 1, oob_is_err=False).then_inc(s_mixg[1], 16)
                    if isinstance(k, int) and k < 2 * NI:
                        e, f = k // 2, k % 2
                        pool.wait_ge(s_blki, 1)
                        pool.indirect_dma_start(out=arena[:, e, f], out_offset=None, in_=cachev[f],
                                                in_offset=bass.IndirectOffsetOnAxis(ap=blk_i[:, e:e + 1], axis=0),
                                                bounds_check=NCACHE - 1, oob_is_err=False).then_inc(s_itemg, 16)

            pool.wait_ge(s_mix[0], 16)
            pool.wait_ge(s_gain, 1)
            expand(wbd[0], wc[0][:, 0, :], s_wbd)
            for n in range(3 * A_UN):
                a_slot(n // A_UN, n % A_UN)
            with pool.Fori(3, NT // A_UN - 1) as i:
                for c in range(A_UN):
                    a_slot(i, c)
            for n in range(NT - A_UN, NT + 6):
                a_slot(n // A_UN, n % A_UN)

            for s in range(NI):
                pool.wait_ge(s_masked, 4 * (s + 1))
                pool.wait_ge(s_stage[s], 16)
                add_rows(nc.gpsimd, s, 1, G // 2, G).then_inc(s_addv, 1)

            def b_slot(i, c):
                if c % GB == 0:
                    g, par = 2 * i + c // GB + 2, (c // GB) % 2
                    if valid(g, NG):
                        if isinstance(g, int) and g < 2:
                            pool.wait_ge(s_patched[g], 32)
                        wait(pool, s_kvt, GB * (g - 1))
                        wait(pool, s_win[par], 32 * (i + 1))
                        nc.gpsimd.tensor_copy(blki[0:WP, par], wini[0:WP, :, bass.ds(g, 1)].rearrange("p k a -> p (k a)")).then_inc(s_bi, 1)
                        wait_first(pool, s_bi, g + 1, s_passed[0])
                        for k in range(2):
                            pool.indirect_dma_start(out=arena[0:WP, par, k], out_offset=None, in_=cachev[k],
                                                    in_offset=bass.IndirectOffsetOnAxis(ap=blki[0:WP, par, 0:1], axis=0),
                                                    bounds_check=NCACHE - 1, oob_is_err=False).then_inc(s_old[par], 16)
                if c % GB == 2:
                    g, par = 2 * i + c // GB + 2, (c // GB) % 2
                    if valid(g, NG):
                        if isinstance(g, int) and g == 0:
                            for s in range(NI):
                                pool.wait_ge(s_patched[s], 32)
                        wait_first(pool, s_old[par], 32 * (i + 2), s_passed[0])
                        for k in range(2):
                            pool.indirect_dma_start(out=arena[0:WP, par, k], out_offset=None, in_=patched[k],
                                                    in_offset=bass.IndirectOffsetOnAxis(ap=blki[0:WP, par, 1:2], axis=0),
                                                    bounds_check=B * NI - 1, oob_is_err=False).then_inc(s_win[par], 16)
                if c % GB == 1:
                    g, par = 2 * i + c // GB + 1, (c // GB + 1) % 2
                    if valid(g, NG):
                        wait(pool, s_s, G * (g - 1))
                        if isinstance(g, int) and g == 0:
                            pool.wait_ge(s_qtc, NT)
                        nc.gpsimd.tensor_copy(qs[par], qt[:, bass.ds(2 * g, 2)].rearrange("p n b h t -> p (n b h t)")).then_inc(s_qs, 1)
                if c % 4 == 0:
                    n, par = 4 * i + c // 4 - 1, (c // 4 - 1) % 2
                    if valid(n, NT):
                        wait(pool, s_l2, n - 1)
                        expand(wbd2[par], wc[1][:, bass.ds(n, 1), :].rearrange("p a d -> p (a d)"), s_w23)

            pool.wait_ge(s_qtc, NT)
            pool.wait_ge(s_addk, 2 * NI)
            pool.wait_ge(s_addv, NI)
            pool.wait_ge(s_mix[1], 16)
            for b in range(2):
                nc.gpsimd.memset(prob[b].rearrange("p g h k -> p (g h k)"), 0.0).then_inc(s_pz, 1)
            run_b(pool, b_slot)

        @block.vector
        def _(dve):
            v = nc.vector
            steps = [0]

            def link(ins):
                steps[0] += 1
                ins.then_inc(s_dve, 1)
                dve.wait_ge(s_dve, steps[0])

            def lag(ins):
                steps[0] += 1
                ins.then_inc(s_dve, 1)
                dve.wait_ge(s_dve, steps[0] - 1)

            dve.wait_ge(s_kv, 16)
            dve.wait_ge(s_cst, 16)
            v.tensor_scalar(f_i, kv_i, BLOCK - 1, None, ALU.bitwise_and)
            link(v.tensor_scalar(s_i, kv_i, int(math.log2(BLOCK)), None, ALU.arith_shift_right))
            v.tensor_copy(kv_f, kv_i)
            v.tensor_copy(f_f, f_i)
            link(v.tensor_copy(s_f, s_i))
            v.tensor_scalar(p_pos, iota(T), kv_f, None, ALU.add)
            v.tensor_scalar(ft, iota(T), f_f, None, ALU.add)
            v.tensor_scalar(low_f, s_f, float(-BLOCK), float(WINDOW - 1), ALU.mult, ALU.add)
            link(v.tensor_scalar(sidx, iota(SLOTS), s_f, float(-SPAN), ALU.add, ALU.add))
            for h in range(GSZ):
                v.tensor_scalar(p_up[:, h], ft, float(WINDOW), None, ALU.add)
                v.tensor_scalar(p_low[:, h], ft, low_f, None, ALU.max)
            link(v.tensor_scalar(sidx, sidx, 0.0, float(NBLK - 1), ALU.max, ALU.min))
            v.sem_inc(s_early, 1)
            dve.wait_ge(s_tab, 16)
            link(v.tensor_copy(tab_f, tab_i))
            for j in range(SLOTS):
                lag(v.scalar_tensor_tensor((pick, chosen[:, 0:NBLK])[j % 2], iota(NBLK), sidx[:, j:j + 1], tab_f,
                                           ALU.is_equal, ALU.mult, accum_out=blk[:, j:j + 1]))
            dve.wait_ge(s_dve, steps[0])
            link(v.tensor_copy(blk_i, blk[:, SPAN:SLOTS]))
            v.sem_inc(s_blk, 1)
            v.sem_inc(s_blki, 1)
            v.memset(eps_c, EPS)
            v.tensor_scalar(f32_f, f_f, float(T), None, ALU.add)
            link(v.tensor_scalar(tmp48, iota(NI * BLOCK), f_f, None, ALU.is_ge))
            v.scalar_tensor_tensor(cov, iota(NI * BLOCK), f32_f, tmp48, ALU.is_lt, ALU.mult)
            v.tensor_scalar(fmask, iota(BLOCK), f_f, None, ALU.is_equal)
            dve.wait_ge(s_scl, 32)
            v.tensor_scalar(gain[:, 0:H, :], scales[:, 0].unsqueeze(1).broadcast_to([P, H, HD]),
                            1.0, 256.0 ** -0.5, ALU.add, ALU.mult)
            link(v.tensor_scalar(gain[:, H:HEADS, :], scales[:, 1].unsqueeze(1).broadcast_to([P, G, HD]),
                                 1.0, None, ALU.add))
            v.sem_inc(s_gain, 1)
            dve.wait_ge(s_itemrow, 16)
            for s in range(NI):
                ins = v.tensor_scalar(same[:, s], item_row, blk[:, SPAN + s:SPAN + s + 1], None, ALU.is_equal)
            link(ins)
            for s in range(NI):
                ins = v.scalar_tensor_tensor(later[:, s], iota(B * NI), cst[:, C_ITEM + s:C_ITEM + s + 1], same[:, s],
                                             ALU.is_lt, ALU.mult)
            link(ins)
            v.sem_inc(s_pairs, 1)
            dve.wait_ge(s_mt, 1)
            link(v.tensor_copy(t1[:, :], ps[3][:, 0:P]))
            link(v.tensor_tensor(ang, t1[:, 0:NT].unsqueeze(2).broadcast_to([P, NT, HD // 2]),
                                 inv.unsqueeze(1).broadcast_to([P, NT, HD // 2]), ALU.mult))
            magic = 1.5 * 2.0 ** 23
            c1 = 6.28125
            c2 = float(np.float32(math.floor((2 * math.pi - c1) * 2.0 ** 21) / 2.0 ** 21))
            c3 = float(np.float32(2 * math.pi - c1 - c2))
            link(v.tensor_scalar(turn, ang, 1.0 / (2 * math.pi), magic, ALU.mult, ALU.add))
            link(v.tensor_scalar(turn, turn, magic, None, ALU.subtract))
            for cc in (c1, c2, c3):
                link(v.scalar_tensor_tensor(ang, turn, -cc, ang, ALU.mult, ALU.add))
            lim = 3.1415925
            link(v.tensor_scalar(ang, ang, -lim, lim, ALU.max, ALU.min))
            link(v.scalar_tensor_tensor(turn, ang, -1.0, ang, ALU.mult, ALU.max))
            link(v.tensor_scalar(turn, turn, -1.0, math.pi / 2, ALU.mult, ALU.add))
            v.sem_inc(s_red, 1)
            dve.wait_ge(s_w23p, 1)
            link(v.tensor_tensor(wsubj[:, 3].rearrange("c s d -> c (s d)"), ps[6][0:T, 0:SUBJ * T],
                                 wsubj[:, 0].rearrange("c s d -> c (s d)"), ALU.add))
            v.sem_inc(s_w23s, 1)
            link(v.tensor_tensor(wsubj[:, 3], wsubj[:, 3], wsubj[:, 2], ALU.add))
            v.sem_inc(s_w23s, 1)
            dve.wait_ge(s_cnt, 1)
            v.scalar_tensor_tensor(wins, ps[0][:, 0:48], 0.0, cov, ALU.is_equal, ALU.mult)
            v.tensor_scalar(keep, ps[1][:, 0:48], 0.0, None, ALU.is_equal)
            link(v.scalar_tensor_tensor(last_num, ps[2][:, 0:B * NI], 0.0, iota(B * NI, 1), ALU.is_equal, ALU.mult))
            v.sem_inc(s_counted, 1)
            for j in range(SLOTS):
                lag(v.scalar_tensor_tensor((chosen, spread[:, 0:B * NI])[j % 2], item_row, blk[:, j:j + 1], last_num,
                                           ALU.is_equal, ALU.mult, accum_out=rep[:, j:j + 1]))
            dve.wait_ge(s_dve, steps[0])
            v.memset(p_win.rearrange("p k j -> p (k j)"), FAR)
            v.tensor_scalar(hit, rep, 0.0, None, ALU.is_gt)
            v.tensor_scalar(base, rep[:, SPAN:SLOTS], float(BLOCK), -float(BLOCK) - FAR, ALU.mult, ALU.add)
            link(v.tensor_scalar(miss, rep, 0.0, None, ALU.is_equal))
            v.scalar_tensor_tensor(p_win[:, 0, 0:SLOTS], hit, FAR, blk, ALU.mult, ALU.add)
            for s in range(NI):
                v.scalar_tensor_tensor(cell[:, 16 * s:16 * s + 16], iota(BLOCK), base[:, s:s + 1],
                                       wins[:, 16 * s:16 * s + 16], ALU.add, ALU.mult)
            link(v.scalar_tensor_tensor(miss, miss, FAR, rep, ALU.mult, ALU.add))
            v.tensor_scalar(p_win[:, 1, 0:SLOTS], miss, -1.0, None, ALU.add)
            lap = cell[:, 0:T].unsqueeze(2).broadcast_to([P, T, BLOCK])
            lap = bass.AP(tensor=lap.tensor, offset=lap.offset, ap=[lap.ap[0], lap.ap[1], [1, BLOCK]])
            link(v.tensor_tensor(spread.rearrange("p (t f) -> p t f", f=BLOCK), lap,
                                 fmask.unsqueeze(1).broadcast_to([P, T, BLOCK]), ALU.mult))
            link(v.tensor_reduce(p_tok, spread.rearrange("p (t f) -> p t f", f=BLOCK), AX.X, ALU.add))
            link(v.tensor_scalar(p_tok, p_tok, FAR, None, ALU.add))
            v.sem_inc(s_pack, 1)

            def late_indices():
                dve.wait_ge(s_mt, 2)
                link(v.tensor_copy(t2[:, :], ps[7][:, 0:P]))
                v.tensor_copy(toki[:, :], t2[:, 0:NT])
                v.tensor_scalar(bounds[:, :, 0], t1[:, 32:96], MASKED, None, ALU.mult)
                v.tensor_copy(wini[:, :, :].rearrange("p k n -> p (k n)"), t2[:, 96:96 + 2 * NG])
                link(v.tensor_scalar(bounds[:, :, 1], t2[:, 32:96], 1.0, MASKED, ALU.add, ALU.mult))
                link(v.tensor_tensor(bounds[:, :, 2], bounds[:, :, 0], bounds[:, :, 1], ALU.subtract))
                v.sem_inc(s_tidx, 1)

            def mask_items(m):
                s, k, h = m // 4, (m // 2) % 2, m % 2
                if m == 0:
                    dve.wait_ge(s_itemg, 32 * NI)
                o = arena[:, s, k].rearrange("p (g o d) -> p g o d", g=G, o=BLOCK)[:, 2 * h:2 * h + 2]
                mask = keep[:, 16 * s:16 * s + 16].unsqueeze(1).broadcast_to([P, 2, BLOCK])
                v.tensor_tensor(o, o, mask.unsqueeze(3).broadcast_to([P, 2, BLOCK, HD]), ALU.mult).then_inc(s_masked, 1)


            def a_slot(i, c):
                k, k5 = A_UN * i + c - 4, A_UN * i + c - 5
                b, b5, r5 = (c - 4) % 2, (c - 5) % 2, (c - 5) % 4
                if valid(k, NT):
                    dve.wait_ge(s_st, k + 1)
                    v.reciprocal(st[b][:, 2 * HEADS:3 * HEADS], st[b][:, HEADS:2 * HEADS]).then_inc(s_rc, 1)
                if valid(k5, NT):
                    q4 = qg[b5].rearrange("p (h e d) -> p h e d", e=2, d=HD // 2)
                    swapped = bass.AP(tensor=q4.tensor, offset=q4[:, :, 1].offset, ap=[q4.ap[0], q4.ap[1], [-(HD // 2), 2], q4.ap[3]])
                    sn = sin[:, k5].unsqueeze(1).broadcast_to([P, HEADS, 2, HD // 2])
                    dve.wait_ge(s_qg, k5 + 1)
                    if isinstance(k5, int) and k5 == 0:
                        dve.wait_ge(s_trig, 3)
                    wait(dve, s_qr, k5 - 1)
                    v.tensor_tensor(rb[b5].rearrange("p (h e d) -> p h e d", e=2, d=HD // 2), swapped, sn, ALU.mult).then_inc(s_rb, 1)
                if valid(k, NT):
                    dve.wait_ge(s_rc, k + 1)
                    wait(dve, s_qg, k - 1)
                    v.tensor_tensor(qn[b].rearrange("p (h d) -> p h d", d=HD),
                                    psq[(c - 4) % 4][:, 0:QK].rearrange("p (h d) -> p h d", d=HD),
                                    st[b][:, 2 * HEADS:3 * HEADS].unsqueeze(2).broadcast_to([P, HEADS, HD]),
                                    ALU.mult).then_inc(s_qn, 1)
                if valid(k5, NT):
                    cs = cos[:, k5, :].unsqueeze(1).broadcast_to([P, 2 * HEADS, HD // 2])
                    v.tensor_tensor(ra[b5].rearrange("p (h d) -> p h d", d=HD // 2), qg[b5].rearrange("p (h d) -> p h d", d=HD // 2),
                                    cs, ALU.mult).then_inc(s_ra, 1)
                k = A_UN * i + c - 3
                b = (c - 3) % 2
                if valid(k, NT):
                    dve.wait_ge(s_sq, k + 1)
                    v.tensor_reduce(st[b][:, 0:HEADS], sq[b].rearrange("p (h d) -> p h d", d=HD), AX.X, ALU.add).then_inc(s_ss, 1)
                k = A_UN * i + c
                if isinstance(k, int) and k == 5:
                    late_indices()
                if valid(k, NT):
                    dve.wait_ge(s_l0, k + 1)
                    wait(dve, s_xt, k - 1)
                    wait(dve, s_xc, k - 1)
                    v.tensor_tensor(x1s[c % 2], psl[c % 2][:, 0:D], xall[:, k, :], ALU.add).then_inc(s_x1, 1)
                if valid(k5, NT):
                    dve.wait_ge(s_rb, k5 + 1)
                    dve.wait_ge(s_ra, k5 + 1)
                    wait(dve, s_scat[r5], 16 * (i + (c - 9) // 4 + 1))
                    wait(dve, s_qt, k5 - 3)
                    v.tensor_tensor(qkvr[r5][:, 0:QK], ra[b5], rb[b5], ALU.add).then_inc(s_qr, 1)

            for n in range(3 * A_UN):
                a_slot(n // A_UN, n % A_UN)
            with dve.Fori(3, NT // A_UN - 1) as i:
                for c in range(A_UN):
                    a_slot(i, c)
            for n in range(NT - A_UN, NT + 6):
                a_slot(n // A_UN, n % A_UN)

            for m in range(4 * NI - 4):
                mask_items(m)
            for s in range(NI):
                if s == 1:
                    for m in range(4 * NI - 4, 4 * NI):
                        mask_items(m)
                dve.wait_ge(s_masked, 4 * (s + 1))
                dve.wait_ge(s_stage[s], 16)
                add_rows(v, s, 0, 0, G).then_inc(s_addk, 1)
                add_rows(v, s, 1, 0, G // 2).then_inc(s_addk, 1)
            dve.wait_ge(s_addv, NI)

            def b_slot(i, c):
                U = 16 * i + c + 1
                b = (c + 1) % 2
                if valid(U, NU):
                    dve.wait_ge(s_mk, 2 * (4 * i + (c + 1) // 4) + 2)
                    wait(dve, s_e, U - 1)
                    wait_first(dve, s_s, GB * i + (c + 1) // 2 + 1, s_passed[2])
                    for q in range(2):
                        v.tensor_tensor_reduce(smx[b][:, q], pss[(c + 1) % 4][:, KEYS * q:KEYS * (q + 1)],
                                               msk[((c + 1) // 4) % 2][:, KEYS * q:KEYS * (q + 1)], -1.0, MASKED * 256,
                                               ALU.add, ALU.min, accum_out=nmax[b][:, q:q + 1]).then_inc(s_sm, 1)
                w = (c + 1) % GB
                g, par = 2 * i + (c + 1) // GB + 1, ((c + 1) // GB + 1) % 2
                if valid(g, NG) and w >= 4:
                    dve.wait_ge(s_kvt, GB * g + w + 1)
                    wait(dve, s_pv, GB * (g - 1))
                    v.transpose(vkeys[:, par, :, HD * (w - 4):HD * (w - 3)], window_columns(window_bank(i, c)[0])).then_inc(s_vc, 1)
                if c % 4 == 0:
                    n, b = 4 * i + c // 4 - 1, (c // 4 - 1) % 2
                    if valid(n, NT):
                        dve.wait_ge(s_e, 4 * n + 4)
                        v.reciprocal(rinv[b], rsum[b]).then_inc(s_rl, 1)
                U = 16 * i + c
                b = c % 2
                if valid(U, NU) and c % 4 != 3:
                    dve.wait_ge(s_pt, U + 1)
                    wait(dve, s_pv, U - 1)
                    v.tensor_copy(pts[b].rearrange("p g k -> p (g k)"), pspt[:, :]).then_inc(s_pc[b], 1)
                if c % 4 == 0:
                    n, b = 4 * i + c // 4 - 1, (c // 4 - 1) % 2
                    if valid(n, NT):
                        dve.wait_ge(s_pv, 4 * n + 4)
                        dve.wait_ge(s_rl, n + 1)
                        wait(dve, s_ot, n - 1)
                        for e in range(2):
                            r = slice(64 * e, 64 * e + 64)
                            v.tensor_tensor(on[b][r].rearrange("p (g d) -> p g d", g=2 * G),
                                            pso[r].rearrange("p (g e d) -> p g e d", g=2 * G, e=2)[:, :, e],
                                            rinv[b][r].unsqueeze(2).broadcast_to([64, 2 * G, HD]), ALU.mult).then_inc(s_on, 1)
                if c % 4 == 0:
                    n, b = 4 * i + (c - 8) // 4, ((c - 8) // 4) % 2
                    if valid(n, NT):
                        dve.wait_ge(s_l2, n + 1)
                        wait(dve, s_out[b], 16 * (2 * i + ((c - 8) // 4 - 2) // 2 + 1))
                        v.scalar_tensor_tensor(x4[b], psw[1], t1[:, bass.ds(96 + n, 1)], x2[b], ALU.add, ALU.add).then_inc(s_x4, 1)
                if c % 4 == 3:
                    n, par = 4 * i + c // 4 + 2, (c // 4) % 2
                    if valid(n, NT):
                        def bound(q, k):
                            return bounds[:, bass.ds(2 * n + q, 1), k:k + 1].rearrange("p a k -> p (a k)")
                        wait(dve, s_mk, 2 * n)
                        for q in range(2):
                            v.tensor_scalar(mska[:, q], kappa, bound(q, 0), bound(q, 2), ALU.max, ALU.subtract).then_inc(s_ma, 1)
                        wait(dve, s_sm, 8 * n - 8)
                        dve.wait_ge(s_ma, 2 * n + 2)
                        for q in range(2):
                            v.scalar_tensor_tensor(msk[par][:, KEYS * q:KEYS * (q + 1)], kappa, bound(q, 1), mska[:, q],
                                                   ALU.min, ALU.subtract).then_inc(s_mk, 1)
                if c % 4 == 2:
                    n, b = 4 * i + (c - 6) // 4, ((c - 6) // 4) % 2
                    if valid(n, NT):
                        dve.wait_ge(s_wo, n + 1)
                        wait(dve, s_x4, n - 1)
                        wait(dve, s_l2, n - 1)
                        v.tensor_tensor(x2[b], psw[0], xall[:, bass.ds(n, 1), :].rearrange("p a d -> p (a d)"), ALU.add).then_inc(s_x2, 1)

            run_b(dve, b_slot)

        @block.scalar
        def _(act):
            a = nc.scalar
            act.dma_start(cst[:, :], consts).then_inc(s_cst, 16)
            act.dma_start(scales[:, 0], q_scale.partition_broadcast(P)).then_inc(s_scl, 16)
            act.dma_start(scales[:, 1], k_scale.partition_broadcast(P)).then_inc(s_scl, 16)
            for k, w in enumerate((w2, w2t, w3)):
                act.dma_start(wsubj[:, k], w.rearrange("s c d -> c s d")).then_inc(s_wsubj, 16)
            act.dma_start(xall[:, 0:NT // 4, :], xv[:, 0:NT // 4, :]).then_inc(s_x[0], 16)
            act.dma_start(wqkv_sb[:, :, :], wqkv).then_inc(s_wts, 16)
            act.dma_start(wo_sb[:, :, :], wo).then_inc(s_wts, 16)
            act.wait_ge(s_itemrow, 16)
            act.wait_ge(s_mix[0], 16)
            act.wait_ge(s_zero, 1)
            for s in range(NI - 1):
                act.dma_start(rowsv[s], zero_row.unsqueeze(1).broadcast_to([P, BLOCK, 2 * G * HD])).then_inc(s_zeroed, 16)
            act.wait_ge(s_red, 1)
            a.activation(sin[:, :, 0], ang, ACT.Sin, scale=-1.0).then_inc(s_trig, 1)
            act.wait_ge(s_trig, 1)
            a.activation(sin[:, :, 1], ang, ACT.Sin).then_inc(s_trig, 1)
            a.activation(cos[:, :, :], turn, ACT.Sin).then_inc(s_trig, 1)

            def a_slot(i, c):
                k = A_UN * i + c - 1
                b = (c - 1) % 2
                if valid(k, NT):
                    act.wait_ge(s_xt, k + 1)
                    wait(act, s_qkv, k - 1)
                    a.copy(x1t[b], psx[:, 0:D].rearrange("p (c t) -> p c t", c=2)).then_inc(s_xtc, 1)
                k = A_UN * i + c - 3
                b, r = (c - 3) % 2, (c - 3) % 4
                if valid(k, NT):
                    wait(act, s_scat[r], 16 * (i + (c - 7) // 4 + 1))
                    a.copy(qkvr[r][:, QK:QKV], psq[r][:, QK:QKV]).then_inc(s_v, 1)
                    act.wait_ge(s_ss, k + 1)
                    wait(act, s_rc, k - 1)
                    a.activation(st[b][:, HEADS:2 * HEADS], st[b][:, 0:HEADS], ACT.Sqrt, bias=eps_c, scale=1.0 / HD).then_inc(s_st, 1)
                k = A_UN * i + c
                if valid(k, NT):
                    act.wait_ge(s_x1, k + 1)
                    a.copy(xall[:, k, :], x1s[c % 2]).then_inc(s_xc, 1)
                k = A_UN * i + c - 2
                b = (c - 2) % 2
                if valid(k, NT):
                    act.wait_ge(s_qkv, k + 1)
                    wait(act, s_ss, k - 1)
                    a.activation(sq[b], psq[(c - 2) % 4][:, 0:QK], ACT.Square).then_inc(s_sq, 1)
                k = A_UN * i + c - 6
                b = (c - 6) % 2
                if valid(k, NT):
                    act.wait_ge(s_qt, k + 1)
                    a.copy(qt[:, k].rearrange("p b h t -> p h b t"),
                           psqt[:, 0:GSZ * P].rearrange("p (h b t) -> p h b t", h=GSZ, b=TB)).then_inc(s_qtc, 1)

            for n in range(3 * A_UN):
                a_slot(n // A_UN, n % A_UN)
            with act.Fori(3, NT // A_UN - 1) as i:
                for c in range(A_UN):
                    a_slot(i, c)
            for n in range(NT - A_UN, NT + 6):
                a_slot(n // A_UN, n % A_UN)

            act.wait_ge(s_pz, 2)

            def b_slot(i, c):
                w = (c + 1) % GB
                g, par = 2 * i + (c + 1) // GB + 1, ((c + 1) // GB + 1) % 2
                if valid(g, NG) and w < 4:
                    act.wait_ge(s_kvt, GB * g + w + 1)
                    wait(act, s_kd[(par + 1) % 2], 256 * (i + (c + 1) // 16 + 1))
                    a.copy(ka[:, w].rearrange("p (m o j) -> p m o j", m=2 * GB, o=4),
                           window_bank(i, c)[0][:, 0:4 * WPX].rearrange("p (o m) -> p o m", o=4)[:, :, 0:WP]
                           .rearrange("p o (m j) -> p m o j", j=JH)).then_inc(s_kc, 1)
                U = 16 * i + c + 1
                b = (c + 1) % 2
                if valid(U, NU):
                    n, g = 4 * i + (c + 1) // 4, (c + 1) % G
                    act.wait_ge(s_sm, 2 * U + 2)
                    wait(act, s_pt, U - 1)
                    wait(act, s_rl, n - 1)
                    for q in range(2):
                        e = a.activation(prob[b][:, q].rearrange("p h (o j) -> p (h o) j", j=8)[:, :, 0:JH],
                                         smx[b][:, q].rearrange("p (o j) -> p o j", j=JH), ACT.Exp,
                                         bias=nmax[b][:, q:q + 1], scale=-1.0,
                                         accum_out=rsum[((c + 1) // 4) % 2][:, G * q + g:G * q + g + 1])
                    e.then_inc(s_e, 1)
                U = 16 * i + c
                b = c % 2
                if valid(U, NU) and c % 4 == 3:
                    act.wait_ge(s_pt, U + 1)
                    wait(act, s_pv, U - 1)
                    a.copy(pts[b].rearrange("p g k -> p (g k)"), pspt[:, :]).then_inc(s_pc[1], 1)
                if c % 4 == 1:
                    n, b = 4 * i + (c - 5) // 4, ((c - 5) // 4) % 2
                    if valid(n, NT):
                        act.wait_ge(s_ot, n + 1)
                        wait(act, s_wo, n - 1)
                        a.copy(ot[b], psot.rearrange("p (b h t) -> p h b t", b=TB, h=GSZ)).then_inc(s_oc, 1)

            run_b(act, b_slot)

        @block.tensor
        def _(pe):
            mm = nc.tensor.matmul
            pe.wait_ge(s_cst, 16)
            pe.wait_ge(s_m1, 16)
            nc.tensor.transpose(ps[3][:, 0:P], m1, ident).then_inc(s_mt, 1)
            pe.wait_ge(s_wsubj, 48)
            for s in range(SUBJ):
                last = mm(ps[6][0:T, T * s:T * (s + 1)], wsubj[:, 1, s], wsubj[:, 2, s], start=True, stop=True)
            last.then_inc(s_w23p, 1)
            pe.wait_ge(s_pairs, 1)
            for m, bank in ((later, ps[0]), (same, ps[1])):
                for s in range(NI):
                    for r in range(NI):
                        mm(bank[:, 16 * s:16 * s + 16], m[:, r].rearrange("p (b s) -> p s b", s=NI)[:, s],
                           cov[:, 16 * r:16 * r + 16], start=(r == 0), stop=(r == NI - 1))
            pe.wait_ge(s_ones, 1)
            for r in range(NI):
                last = mm(ps[2][:, 0:B * NI], ones, later[:, r], start=(r == 0), stop=(r == NI - 1))
            last.then_inc(s_cnt, 1)
            pe.wait_ge(s_wts, 32)
            pe.wait_ge(s_x[0], 16)
            pe.wait_ge(s_counted, 1)

            def a_slot(i, c):
                k = A_UN * i + c
                b = c % 2
                if isinstance(k, int) and k == 5:
                    pe.wait_ge(s_m, 48)
                    nc.tensor.transpose(ps[7][:, 0:P], m2, ident).then_inc(s_mt, 1)
                if isinstance(k, int) and k == NT // 4:
                    pe.wait_ge(s_x[1], 16)
                if isinstance(k, int) and k == 3 * A_UN - 1:
                    pe.wait_ge(s_x[2], 16)
                if valid(k, NT):
                    pe.wait_ge(s_wbd, k + 1)
                    wait(pe, s_x1, k - 1)
                    mm(psl[b][:, 0:D], wbd[b], xall[:, k, :], start=True, stop=True).then_inc(s_l0, 1)
                k = A_UN * i + c - 1
                b = (c - 1) % 2
                if valid(k, NT):
                    pe.wait_ge(s_x1, k + 1)
                    wait(pe, s_xtc, k)
                    nc.tensor.transpose(psx[:, 0:P], x1s[b][:, 0:P], ident)
                    nc.tensor.transpose(psx[:, P:2 * P], x1s[b][:, P:2 * P], ident).then_inc(s_xt, 1)
                k = A_UN * i + c - 2
                b = (c - 2) % 2
                if valid(k, NT):
                    pe.wait_ge(s_xtc, k + 1)
                    wait(pe, s_qn, k - 3)
                    wait(pe, s_v, k - 3)
                    for d in range(2):
                        last = mm(psq[(c - 2) % 4][:, :], x1t[b][:, d], wqkv_sb[:, d, :], start=(d == 0), stop=(d == 1))
                    last.then_inc(s_qkv, 1)
                k = A_UN * i + c - 6
                b, r = (c - 6) % 2, (c - 6) % 4
                if valid(k, NT):
                    pe.wait_ge(s_qr, k + 1)
                    wait(pe, s_qtc, k)
                    if isinstance(k, int) and k == 0:
                        pe.wait_ge(s_tidx, 1)
                    q = qkvr[r][:, 0:H * HD].rearrange("p (h e) -> p h e", h=GSZ)
                    for h in range(GSZ):
                        last = nc.tensor.transpose(psqt[:, P * h:P * (h + 1)], q[:, h], ident)
                    last.then_inc(s_qt, 1)

            for n in range(3 * A_UN):
                a_slot(n // A_UN, n % A_UN)
            with pe.Fori(3, NT // A_UN - 1) as i:
                for c in range(A_UN):
                    a_slot(i, c)
            for n in range(NT - A_UN, NT + 6):
                a_slot(n // A_UN, n % A_UN)

            pe.wait_ge(s_qtc, NT)

            def keys_of(r, q, bb):
                return ktr[r:r + HD, q, 2 * bb:2 * bb + 2]

            BURSTS = {(-1, 13): 8, (0, 0): 4}

            def b_slot(i, c):
                kv_bank, first_group = window_bank(i, c)
                if isinstance(i, int) and (i, c) in BURSTS:
                    for k in range(BURSTS[i, c]):
                        mm(ps[7][:, :], ident, xall[:, 0:2, :].rearrange("p n d -> p (n d)"), start=True, stop=True)
                if c % 2 == 1:
                    V = GB * i + (c + 3) // 2
                    if valid(V, NU // 2):
                        q = ((c + 3) // GB) % 2
                        g8 = 2 * i + (c + 3) // GB
                        pe.wait_ge(s_qs, g8 + 1)
                        pe.wait_ge(s_kd[q], 256 * (i + (c + 3) // 16 + 1))
                        wait(pe, s_sm, 4 * (V - 1))
                        for k in range(2):
                            for u in range(2):
                                for e in range(2):
                                    r = HD * ((c + 3 + u) % G)
                                    bb = TB * (((c + 3) % GB) // 4) + 2 * k + e
                                    last = mm(pss[(c + 3 + u) % 4][64 * e:64 * e + 64, KEYS * k:KEYS * (k + 1)],
                                              qs[q][r:r + HD, 64 * bb:64 * bb + 64],
                                              keys_of(r, q, bb), start=True, stop=True)
                        last.then_inc(s_s, 1)
                w = (c + 1) % GB
                g8, par = 2 * i + (c + 1) // GB + 1, ((c + 1) // GB + 1) % 2
                if valid(g8, NG):
                    if w == 0:
                        pe.wait_ge(s_win[par], 32 * (i + ((c + 1) // GB + 1) // 2 + 1))
                    if first_group:
                        if 2 <= w < 6:
                            pe.wait_ge(s_kc, w - 1)
                        elif w >= 6:
                            pe.wait_ge(s_vc, w - 5)
                    elif w == 0:
                        wait(pe, s_vc, 4 * g8)
                    elif w < 5:
                        pe.wait_ge(s_kc, 4 * g8 + w)
                    else:
                        pe.wait_ge(s_vc, 4 * g8 + w - 4)
                    for o in range(4):
                        first = BLOCK * HD * (w % 4) + P * o
                        src = arena[0:WPX, par, w // 4, first:first + P]
                        last = nc.tensor.transpose(kv_bank[:, WPX * o:WPX * (o + 1)], src, ident[0:WPX, 0:WPX])
                    last.then_inc(s_kvt, 1)
                U = 16 * i + c
                b = c % 2
                if valid(U, NU):
                    pe.wait_ge(s_e, U + 1)
                    wait(pe, s_pc[1 - b], GB * i + (c + 1) // 2)
                    for k in range(4):
                        last = nc.tensor.transpose(pspt[:, P * k:P * (k + 1)], prob[b][:, k // 2, k % 2], ident)
                    last.then_inc(s_pt, 1)
                U = 16 * i + c - 1
                b, q = (c - 1) % 2, ((c - 1) // GB) % 2
                if valid(U, NU):
                    n, g = 4 * i + (c - 1) // 4, (c - 1) % G
                    pe.wait_ge(s_pc[b], GB * i + (c - 1) // 2 + 1)
                    pe.wait_ge(s_vc, 4 * (2 * i + (c - 1) // GB) + 4)
                    if g == 0:
                        wait(pe, s_on, 2 * n)
                    for k in range(2):
                        col = 2 * HD * (G * k + g)
                        bb = TB * (((c - 1) % GB) // 4) + 2 * k
                        for h in range(2):
                            last = mm(pso[:, col:col + 2 * HD].rearrange("p (e d) -> p e d", e=2), pts[b][:, 2 * k + h],
                                      vkeys[:, q, 2 * bb + h:2 * bb + h + 3:2, HD * g:HD * (g + 1)], start=(h == 0), stop=(h == 1))
                    last.then_inc(s_pv, 1)
                if c % 4 == 1:
                    n, b = 4 * i + (c - 5) // 4, ((c - 5) // 4) % 2
                    if valid(n, NT):
                        pe.wait_ge(s_on, 2 * n + 2)
                        wait(pe, s_x4, n)
                        for k in range(2):
                            last = nc.tensor.transpose(psot[:, P * k:P * (k + 1)], on[b][:, P * k:P * (k + 1)], ident)
                        last.then_inc(s_ot, 1)
                if c % 4 == 2:
                    n, b = 4 * i + (c - 6) // 4, ((c - 6) // 4) % 2
                    if valid(n, NT):
                        pe.wait_ge(s_oc, n + 1)
                        for h in range(GSZ):
                            last = mm(psw[0], ot[b][:, h].rearrange("p b t -> p (b t)"), wo_sb[:, h, :], start=(h == 0), stop=(h == 1))
                        last.then_inc(s_wo, 1)
                if c % 4 == 3:
                    n, b = 4 * i + (c - 7) // 4, ((c - 7) // 4) % 2
                    if valid(n, NT):
                        pe.wait_ge(s_x2, n + 1)
                        pe.wait_ge(s_w23, n + 1)
                        mm(psw[1], wbd2[b], x2[b], start=True, stop=True).then_inc(s_l2, 1)

            run_b(pe, b_slot)


def kernel(**inputs):
    import concourse.bacc as _bacc
    from concourse import mybir as _mybir
    from concourse.bass_utils import run_bass_kernel_spmd as _run

    a = {k: np.ascontiguousarray(v) for k, v in inputs.items()}
    wqkv = np.concatenate([a["L1_cond_Wq"].reshape(G, GSZ, HD, D).transpose(1, 0, 2, 3).reshape(H * HD, D), a["L1_cond_Wk"], a["L1_cond_Wv"]], 0).T
    wqkv = wqkv.reshape(2, P, QKV).transpose(1, 0, 2)
    wo = a["L1_cond_Wo"].T.reshape(G, GSZ, HD, D).transpose(0, 2, 1, 3).reshape(P, GSZ, D)
    arrays = {
        "x": a["x"], "conditions": a["itok_B_1_198"], "tables": a["itok_Bx257_0_4111"], "kv_lens": a["itok_B_37_3939"],
        "subjects": a["itok_B_0_7"], "bias": a["fside_8xS_0"], "w0": a["L0_cond_weights"], "w2": a["L2_cond_weights"],
        "w2t": a["L2_cond_weights"].transpose(0, 2, 1),
        "w3": a["L3_cond_weights"], "wqkv": wqkv, "wo": wo, "q_scale": a["L1_cond_q_norm_scale"],
        "k_scale": a["L1_cond_k_norm_scale"], "k_cache": a["L1_cond_k_blocks"], "v_cache": a["L1_cond_v_blocks"],
        "consts": constants(),
    }
    arrays = {k: np.ascontiguousarray(v) for k, v in arrays.items()}
    nc = _bacc.Bacc("TRN2", target_bir_lowering=False, num_devices=1)
    args = [nc.dram_tensor(k, v.shape, _mybir.dt.from_np(v.dtype), kind="ExternalInput").ap() for k, v in arrays.items()]
    out = nc.dram_tensor("out", (B, T, D), F32, kind="ExternalOutput").ap()
    build(nc, *args, out)
    r = _run(nc, [arrays], core_ids=[0])
    return r.results[0]["out"]
```
